# Optimizing a Trainium2 kernel written in Bass

```python
import numpy as np
import jax
import jax.numpy as jnp

def _softmax(x, axis=-1):
    return jax.nn.softmax(x, axis=axis)

def _gelu(x):
    return jax.nn.gelu(x, approximate=True)

def _silu(x):
    return jax.nn.silu(x)

def _sigmoid(x):
    return jax.nn.sigmoid(x)

def _layernorm(x, axis=-1, eps=1e-05):
    m = jnp.mean(x, axis=axis, keepdims=True)
    v = jnp.var(x, axis=axis, keepdims=True)
    return (x - m) / jnp.sqrt(v + eps)

def _scatter_add(tgt, idx, src, axis=0):
    return tgt.at[idx].add(src)

def _segment_sum(src, seg, n):
    return jax.ops.segment_sum(src, seg, n)
kernel_name = 'mk_gnn_resnorm_d1_gnn_r32_f15448'

def setup_inputs(seed: int=0):
    np.random.seed(seed)
    _w = jnp.asarray

    def _rec_inputs():
        import jax
        import jax.numpy as jnp
        _gk = jax.random.key(seed)
        x = -0.0001126 + 1 * jax.random.normal(jax.random.fold_in(_gk, 1), (3125, 256), jnp.float32)
        src = jax.random.randint(jax.random.fold_in(_gk, 2), (50000,), 0, 3125, jnp.int32)
        dst = jax.random.randint(jax.random.fold_in(_gk, 3), (50000,), 0, 3125, jnp.int32)
        _o = jnp.argsort(dst, stable=True)
        src = src[_o]
        dst = dst[_o]
        edge_type_8 = jax.random.randint(jax.random.fold_in(_gk, 12), (50000,), 0, 8, jnp.int32)
        return (x, src, dst, edge_type_8)
    x, src, dst, edge_type_8 = _rec_inputs()

    def _L0_gnn_setup():
        import jax, jax.numpy as jnp
        import numpy as np
        N, E, R, H, D = (30000, 9375, 8, 8, 32)
        IN_F = 256
        NEG_SLOPE = 0.2
        key = jax.random.key(seed)
        k = jax.random.split(key, 6)
        x = jax.random.normal(k[0], (N, IN_F), dtype=jnp.float32)
        W = jax.random.normal(k[1], (R, H * D, IN_F), dtype=jnp.float32) * 0.05
        attn_src = jax.random.normal(k[2], (H, D), dtype=jnp.float32) * 0.1
        attn_dst = jax.random.normal(k[3], (H, D), dtype=jnp.float32) * 0.1
        edge_index = jax.random.randint(k[4], (2, E), 0, N, dtype=jnp.int64) if jax.config.read('jax_enable_x64') else jax.random.randint(k[4], (2, E), 0, N, dtype=jnp.int32)
        edge_type = jax.random.randint(k[5], (E,), 0, R, dtype=edge_index.dtype)
        return dict(x=x, W=W, attn_src=attn_src, attn_dst=attn_dst, edge_index=edge_index, edge_type=edge_type)
    _L0_gnn_all = _L0_gnn_setup()
    _L0_gnn_in = {k: v for k, v in _L0_gnn_all.items() if k in ('W', 'attn_src', 'attn_dst')}
    del _L0_gnn_all
    return {'x': x, 'src': src, 'dst': dst, 'edge_type_8': edge_type_8, 'L0_gnn_W': _L0_gnn_in['W'], 'L0_gnn_attn_src': _L0_gnn_in['attn_src'], 'L0_gnn_attn_dst': _L0_gnn_in['attn_dst']}

def reference(x, src, dst, edge_type_8, L0_gnn_W, L0_gnn_attn_src, L0_gnn_attn_dst):
    import jax
    import jax.numpy as jnp

    def _L0_gnn_ref(x, W, attn_src, attn_dst, edge_index, edge_type):
        import jax, jax.numpy as jnp
        import numpy as np
        N, E, R, H, D = (30000, 9375, 8, 8, 32)
        IN_F = 256
        NEG_SLOPE = 0.2
        n = x.shape[0]
        r = W.shape[0]
        h, d = attn_src.shape
        h_all = jnp.einsum('nf,rof->rno', x, W).reshape(r, n, h, d)
        src, dst = (edge_index[0], edge_index[1])
        h_src = h_all[edge_type, src]
        h_dst = h_all[edge_type, dst]
        scores = jnp.einsum('ehd,hd->eh', h_src, attn_src) + jnp.einsum('ehd,hd->eh', h_dst, attn_dst)
        scores = jnp.where(scores > 0, scores, NEG_SLOPE * scores)
        amax = jnp.maximum(jax.ops.segment_max(scores, dst, num_segments=n), 0.0)
        w = jnp.exp(scores - amax[dst])
        denom = jax.ops.segment_sum(w, dst, num_segments=n) + 1e-12
        w = w / denom[dst]
        msg = h_src * w[..., None]
        out = jax.ops.segment_sum(msg, dst, num_segments=n)
        return out.reshape(n, h * d)
    edge_index = jnp.stack([src, dst])
    x = _layernorm(x + _L0_gnn_ref(x, L0_gnn_W, L0_gnn_attn_src, L0_gnn_attn_dst, edge_index, edge_type_8), axis=-1)
    return x

_drawn_inputs = setup_inputs


def setup_inputs(seed=0):
    import zlib

    import numpy as np

    out = dict(_drawn_inputs(seed))
    spreads = {}
    factors = {}
    for name, (base, spread) in spreads.items():
        noise = np.random.default_rng([zlib.crc32(name.encode()), seed]).standard_normal(out[name].shape)
        drawn = base * np.exp(spread * noise) if base else spread * noise
        out[name] = jnp.asarray(drawn.astype(out[name].dtype))
    for name, factor in factors.items():
        out[name] = (out[name] * factor).astype(out[name].dtype)
    return out
```

```python
import numpy as np

N, F = 3125, 256
R, H, D = 8, 8, 32
E = 50000
NEG_SLOPE = 0.2
DENOM_EPS = 1e-12
LN_EPS = 1e-5

P = 128
KT = F // P
WINDOWS = -(-N // P)
TAIL = N - (WINDOWS - 1) * P
EP = 125
T = 4
GE = EP * T
GROUPS = E // GE
STEPS = GROUPS - 1 + WINDOWS
Q = 4
QUADS = STEPS // Q
SLOTS = 3
ROW = F + H
GROW = ROW + H
PRE = 5
PAD = 32
BIG = 1e30
assert GROUPS * GE == E and QUADS * Q == STEPS and PRE * WINDOWS == STEPS + 1
assert (QUADS - 1) % SLOTS == 0 and WINDOWS % 2 == 1


def gnn_kernel(nc, x, src, dst, etype, W, attn_src, attn_dst, out):
    import concourse.bass as bass
    from concourse import mybir
    from contextlib import ExitStack

    ALU = mybir.AluOpType
    ACT = mybir.ActivationFunctionType
    F32 = mybir.dt.float32
    I32 = mybir.dt.int32
    AXX = mybir.AxisListType.X
    ds = bass.ds

    with ExitStack() as ctx:
        def sb(name, shape, dt=F32):
            return ctx.enter_context(nc.sbuf_tensor(name, shape, dt))

        def ps(name, shape):
            return ctx.enter_context(nc.psum_tensor(name, shape, F32))

        def sem(name):
            return ctx.enter_context(nc.semaphore(name))

        def dram(name, shape, dt=F32):
            return nc.dram_tensor(name, shape, dt, kind="Internal").ap()

        table = dram("table", [N * R, ROW])
        rec_d = dram("rec_d", [GROUPS, EP, T * 4], I32)
        brk_d = dram("brk_d", [GROUPS, 2 * GE])
        dstrow_d = dram("dstrow_d", [GROUPS, GE])
        sdst_d = dram("sdst_d", [WINDOWS, P, H * R])
        acc_d = dram("acc_d", [STEPS + 2, P, ROW])

        big = sb("big", [P, SLOTS * Q * T * GROW])
        G = big[0:EP, :].rearrange("p (z c w) -> p z c w", z=SLOTS, w=GROW)
        Wnat = big[:, 0:16 * F].rearrange("p (a f) -> p a f", a=2 * R)
        WT = big[:, 16 * F:16 * F + KT * R * F].rearrange("p (k n) -> p k n", k=KT)
        ident = sb("ident", [P, P])
        ones = sb("ones", [P, P])
        headsel = sb("headsel", [P, 2, H])
        attn_col = sb("attn_col", [P, 2, 2])
        Bd = sb("Bd", [P, 2, 2 * H])
        A = sb("A", [P, KT, 2 * H * R])
        iota_row = sb("iota_row", [P, P], I32)
        iota_col = sb("iota_col", [P, 1], I32)
        pcol = sb("pcol", [P, 1])
        dstE = sb("dstE", [GROUPS, GE], I32)
        srcE = sb("srcE", [GROUPS, GE], I32)
        typE = sb("typE", [GROUPS, GE], I32)
        recE = sb("recE", [GROUPS, GE, 4], I32)
        neE = sb("neE", [GROUPS, GE])
        brkE = sb("brkE", [GROUPS, 2, GE])
        dstF = sb("dstF", [GROUPS, GE])
        wlast = sb("wlast", [GROUPS, 1], I32)
        wlastF = sb("wlastF", [GROUPS, 1])
        glast = sb("glast", [GROUPS, 1])
        cmp = sb("cmp", [GROUPS, STEPS + WINDOWS])
        cnt = sb("cnt", [P, STEPS + WINDOWS])
        win = sb("win", [P, STEPS])
        win128 = sb("win128", [P, STEPS])
        node = sb("node", [P, STEPS])
        keep = sb("keep", [P, STEPS])
        gtab = sb("gtab", [1, STEPS], I32)
        wtab = sb("wtab", [1, STEPS], I32)
        ltab = sb("ltab", [1, WINDOWS], I32)
        xin = sb("xin", [P, 2, F])
        xT = sb("xT", [P, 2, KT, P])
        sdo = sb("sdo", [P, 2, H * R])
        hbuf = sb("hbuf", [P, 2, R, ROW])
        drow = sb("drow", [P, PRE, GE])
        sdw = sb("sdw", [P, PRE, H * R])
        ohT = sb("ohT", [P, 2, GE])
        rec = sb("rec", [EP, STEPS, T, 4], I32)
        idx = sb("idx", [EP, SLOTS, Q * T], I32)
        rmask = sb("rmask", [EP, 2, T, R])
        sdm = sb("sdm", [EP, 2, T * H, R])
        sdS = sb("sdS", [EP, STEPS, T, H])
        sraw = sb("sraw", [EP, T * Q, H])
        s4 = sb("s4", [EP, T, Q, PAD])
        sT = sb("sT", [P, GE])
        fwd = sb("fwd", [P, GE])
        mT = sb("mT", [P, GE])
        brk = sb("brk", [P, 2, 2, GE])
        dif = sb("dif", [EP, T * Q, H])
        onehot = sb("onehot", [EP, 2, T, P])
        M = sb("M", [P, 2, H])
        dab = sb("dab", [P, 2 * H])
        eab = sb("eab", [P, 2 * H])
        accS = sb("accS", [P, 2, ROW])
        tsum = sb("tsum", [P, ROW])
        fin = sb("fin", [P, 2, ROW])
        xres = sb("xres", [P, 2, F])
        rden = sb("rden", [P, 2, H])
        y = sb("y", [P, 2, F])
        st = sb("st", [P, 2, 6])
        mv = sb("mv", [P, 2, 2])
        sd_ = sb("sd_", [P, 2, 1])
        o = sb("o", [P, 2, F])
        eps = sb("eps", [P, 1])

        psX = [ps(f"psX{b}", [P, 512]) for b in range(2)]
        psH = [ps(f"psH{b}", [P, 512]) for b in range(4)]
        psS = ps("psS", [P, 512])
        psD = ps("psD", [P, 512])
        psE = [psS, psD]
        psT, psM = psH[0], psH[1]
        psP = [psH[2], psH[3]]

        edges_in, w_in, attn_in = sem("edges_in"), sem("w_in"), sem("attn_in")
        consts0, consts = sem("consts0"), sem("consts")
        prep = sem("prep")
        rec_out = sem("rec_out")
        cnt_mm, tabs = sem("cnt_mm"), sem("tabs")
        bd_made = sem("bd_made")
        wt_mm, wt_out = sem("wt_mm"), sem("wt_out")
        a_mm, a_out = sem("a_mm"), sem("a_out")
        x_in = [sem(f"x_in{b}") for b in range(2)]
        xt_mm, xt_out = sem("xt_mm"), sem("xt_out")
        sc_mm, sc_out = sem("sc_mm"), sem("sc_out")
        sd_st = [sem(f"sd_st{b}") for b in range(2)]
        h_mm, h_out = sem("h_mm"), sem("h_out")
        h_st = [sem(f"h_st{b}") for b in range(2)]
        drow_in = [sem(f"drow_in{b}") for b in range(PRE)]
        sdw_in = [sem(f"sdw_in{b}") for b in range(PRE)]
        rec_in = [sem(f"rec_in{b}") for b in range(PRE)]
        oht, rm_made, sd_mm, sdm_made, sd_done = sem("oht"), sem("rm_made"), sem("sd_mm"), sem("sdm_made"), sem("sd_done")
        idx_made = sem("idx_made")
        gath = [[sem(f"gath{z}_{g}") for g in range(Q)] for z in range(SLOTS)]
        zeroed = sem("zeroed")
        sraw_made, s4_made = sem("sraw_made"), sem("s4_made")
        sT_mm, sT_out = sem("sT_mm"), sem("sT_out")
        brk_in = [sem(f"brk_in{b}") for b in range(2)]
        fwd_made, mT_made, m_mm = sem("fwd_made"), sem("mT_made"), sem("m_mm")
        dif_made, w_made, first_made = sem("dif_made"), sem("w_made"), sem("first_made")
        oh_made, msg_made, p_mm = sem("oh_made"), sem("msg_made"), sem("p_mm")
        mnew, dab_made, eab_made = sem("mnew"), sem("dab_made"), sem("eab_made")
        t1, t2, acc_made = sem("t1"), sem("t2"), sem("acc_made")
        acc_st = [sem(f"acc_st{b}") for b in range(2)]
        fin_in = [sem(f"fin_in{b}") for b in range(2)]
        ne_made, last_made, cols_made = sem("ne_made"), sem("last_made"), sem("cols_made")
        cmp_made, win_made, pcol_made = sem("cmp_made"), sem("win_made"), sem("pcol_made")
        stats_made, mv_made, rstd_made = sem("stats_made"), sem("mv_made"), sem("rstd_made")
        root_made, mean_made, o_made = sem("root_made"), sem("mean_made"), sem("o_made")
        o_st = [sem(f"o_st{b}") for b in range(2)]

        block = ctx.enter_context(nc.Block())

        SWEEPS = (WINDOWS - 1) // 2

        @block.sync
        def _(sp):
            sp.dma_start(dstE[:, :], dst.rearrange("(g e) -> g e", g=GROUPS)).then_inc(edges_in, 16)
            sp.dma_start(srcE[:, :], src.rearrange("(g e) -> g e", g=GROUPS)).then_inc(edges_in, 16)
            sp.dma_start(typE[:, :], etype.rearrange("(g e) -> g e", g=GROUPS)).then_inc(edges_in, 16)
            for r in range(R):
                sp.dma_start(Wnat[:, 2 * r:2 * r + 2, :], W[r].rearrange("(a o) f -> o a f", a=2)).then_inc(w_in, 16)
            sp.wait_ge(prep, 7)
            sp.dma_start(rec_d.rearrange("g p c -> g (p c)"), recE[:, :, :].rearrange("g e c -> g (e c)")).then_inc(rec_out, 16)
            sp.dma_start(brk_d, brkE[:, :, :].rearrange("g a e -> g (a e)")).then_inc(rec_out, 16)
            sp.dma_start(dstrow_d, dstF[:, :]).then_inc(rec_out, 16)
            sp.wait_ge(rec_out, 48)
            sp.wait_ge(tabs, 7)

            def stage(s, j, cond):
                g = sp.value_load(gtab[0:1, ds(s, 1)], min_val=0, max_val=GROUPS - 1)
                if cond is not None:
                    sp.wait_ge(oht, cond)
                sp.dma_start(rec[:, ds(s, 1), :, :].rearrange("p a t c -> p (a t c)"),
                             rec_d[ds(g, 1), :, :].rearrange("a p c -> p (a c)")).then_inc(rec_in[j], 16)
                sp.dma_start(drow[:, j, :], dstrow_d[ds(g, 1), :].to_broadcast([P, GE])).then_inc(drow_in[j], 16)

            for j in range(PRE):
                stage(j, j, None)
            with sp.Fori(1, WINDOWS - 1) as i:
                for j in range(PRE):
                    stage(i * PRE + j, j, i * PRE + j + 1 - PRE)
            for j in range(PRE - 1):
                s = (WINDOWS - 1) * PRE + j
                stage(s, j, s + 1 - PRE)

            def breaks(q, b):
                for g_ in range(Q):
                    g = sp.value_load(gtab[0:1, ds(q * Q + g_, 1)], min_val=0, max_val=GROUPS - 1)
                    sp.dma_start(brk[g_ * PAD:g_ * PAD + H, b, :, :].rearrange("p a e -> p (a e)"),
                                 brk_d[ds(g, 1), :].to_broadcast([H, 2 * GE])).then_inc(brk_in[b], 16)

            def store_acc(s, b):
                sp.wait_ge(acc_made, s + 3)
                sp.dma_start(acc_d[ds(s, 1), :, :].rearrange("a p c -> p (a c)"), accS[:, b, :]).then_inc(acc_st[b], 16)

            sp.wait_ge(zeroed, 2)
            sp.wait_ge(acc_made, 2)
            for b in range(2):
                sp.dma_start(acc_d[STEPS + b], accS[:, b, :]).then_inc(acc_st[b], 16)
            breaks(0, 0)
            breaks(1, 1)
            for g_ in range(Q):
                store_acc(g_, g_ % 2)
            with sp.Fori(0, (QUADS - 3) // 2) as i:
                for b in range(2):
                    q = i * 2 + b + 2
                    sp.wait_ge(mT_made, q - 1)
                    breaks(q, b)
                    for g_ in range(Q):
                        store_acc((q - 1) * Q + g_, g_ % 2)
            sp.wait_ge(mT_made, QUADS - 2)
            breaks(QUADS - 1, (QUADS - 1) % 2)
            for s in range((QUADS - 2) * Q, STEPS):
                store_acc(s, s % 2)
            for b in range(2):
                sp.wait_ge(acc_st[b], 16 * (STEPS // 2 + 1))

            def load_fin(w, b, rows):
                last = sp.value_load(ltab[0:1, ds(w, 1)], min_val=0, max_val=STEPS - 1)
                sp.dma_start(fin[:, b, :], acc_d[ds(last, 1), :, :].rearrange("a p c -> p (a c)")).then_inc(fin_in[b], 16)
                sp.dma_start(xres[0:rows, b, :], x[ds(w * P, rows), :]).then_inc(fin_in[b], 16)

            def store_out(w, b, rows):
                sp.wait_ge(o_made, w + 1)
                sp.dma_start(out[ds(w * P, rows), :], o[0:rows, b, :]).then_inc(o_st[b], 16)

            load_fin(0, 0, P)
            load_fin(1, 1, P)
            with sp.Fori(0, SWEEPS - 1) as i:
                for b in range(2):
                    store_out(i * 2 + b, b, P)
                    load_fin(i * 2 + b + 2, b, P)
            store_out(WINDOWS - 3, 0, P)
            load_fin(WINDOWS - 1, 0, TAIL)
            store_out(WINDOWS - 2, 1, P)
            store_out(WINDOWS - 1, 0, TAIL)
            sp.wait_ge(o_st[0], 16 * (SWEEPS + 1))
            sp.wait_ge(o_st[1], 16 * SWEEPS)

        @block.gpsimd
        def _(pool):
            nc.gpsimd.memset(ident[:, :], 0.0).then_inc(consts0, 1)
            nc.gpsimd.memset(headsel[:, :, :], 1.0).then_inc(consts0, 1)
            nc.gpsimd.iota(iota_row[:, :], pattern=[[1, P]], base=0, channel_multiplier=0).then_inc(consts, 1)
            nc.gpsimd.iota(iota_col[:, :], pattern=[[1, 1]], base=0, channel_multiplier=1).then_inc(consts, 1)
            nc.gpsimd.memset(ones[:, :], 1.0).then_inc(consts, 1)
            pool.wait_ge(consts0, 2)
            nc.gpsimd.affine_select(out=ident[:, :], in_=ident[:, :], compare_op=ALU.not_equal, fill=1.0,
                                    base=0, pattern=[[-1, P]], channel_multiplier=1).then_inc(consts, 1)
            nc.gpsimd.affine_select(out=headsel[:, :, :], in_=headsel[:, :, :], compare_op=ALU.is_ge, fill=0.0,
                                    base=0, pattern=[[P, 2], [-D, H]], channel_multiplier=1).then_inc(consts0, 1)
            pool.wait_ge(consts0, 3)
            nc.gpsimd.affine_select(out=headsel[:, :, :], in_=headsel[:, :, :], compare_op=ALU.is_ge, fill=0.0,
                                    base=D - 1, pattern=[[-P, 2], [D, H]], channel_multiplier=-1).then_inc(consts, 1)

            def stage_scores(s, j, cond):
                w = pool.value_load(wtab[0:1, ds(s, 1)], min_val=0, max_val=WINDOWS - 1)
                if cond is not None:
                    pool.wait_ge(sd_mm, cond)
                pool.dma_start(sdw[:, j, :], sdst_d[ds(w, 1), :, :].rearrange("a p c -> p (a c)")).then_inc(sdw_in[j], 16)

            pool.wait_ge(tabs, 7)
            for b, n in ((0, SWEEPS + 1), (1, SWEEPS)):
                pool.wait_ge(sd_st[b], 16 * n)
            for j in range(PRE):
                stage_scores(j, j, None)
            with pool.Fori(1, WINDOWS - 1) as i:
                for j in range(PRE):
                    stage_scores(i * PRE + j, j, i * PRE + j + 1 - PRE)
            for j in range(PRE - 1):
                s = (WINDOWS - 1) * PRE + j
                stage_scores(s, j, s + 1 - PRE)

            for j, n in ((0, WINDOWS), (1, WINDOWS), (2, WINDOWS), (3, WINDOWS), (4, WINDOWS - 1)):
                pool.wait_ge(rec_in[j], 16 * n)
            for b, n in ((0, SWEEPS + 1), (1, SWEEPS)):
                pool.wait_ge(h_st[b], 16 * n)

            def gather(q, z, cond, n=None):
                if n is not None:
                    for g in range(Q):
                        pool.wait_ge(gath[z][g], n)
                nc.gpsimd.tensor_copy(idx[:, z, :].rearrange("p (g t) -> p g t", g=Q),
                                      rec[:, ds(q * Q, Q), :, 0]).then_inc(idx_made, 1)
                pool.wait_ge(idx_made, q + 1)
                pool.nop(nofuse=True)
                for g in range(Q):
                    if cond is not None:
                        pool.wait_ge(p_mm, cond + g)
                        pool.nop(nofuse=True)
                    for t in range(T):
                        nc.gpsimd.indirect_dma_start(G[:, z, g * T + t, 0:ROW], None, table,
                                                     bass.IndirectOffsetOnAxis(ap=idx[:, z, g * T + t:g * T + t + 1], axis=0)).then_inc(gath[z][g], 16)
            for z in range(SLOTS):
                gather(z, z, None)
            with pool.Fori(1, QUADS // SLOTS) as i:
                for z in range(SLOTS):
                    gather(i * SLOTS + z, z, (i * SLOTS + z - SLOTS) * Q + 1, i * 16 * T)
            gather(QUADS - 1, 0, (QUADS - 1 - SLOTS) * Q + 1, (QUADS // SLOTS) * 16 * T)

        @block.tensor
        def _(pe):
            pe.wait_ge(consts, 5)
            pe.wait_ge(cmp_made, 2)
            nc.tensor.matmul(psS[:, 0:STEPS + WINDOWS], ones[0:GROUPS, :], cmp[:, :], start=True, stop=True).then_inc(cnt_mm, 1)
            pe.wait_ge(w_in, 16 * R)
            pe.wait_ge(bd_made, 2)
            for r in range(R):
                for k in range(KT):
                    for a in range(2):
                        mm = nc.tensor.matmul(psD[:, (k * R + r) * 16:(k * R + r) * 16 + 16],
                                              Wnat[:, 2 * r + a, k * P:(k + 1) * P], Bd[:, a, :], start=a == 0, stop=a == 1)
            mm.then_inc(a_mm, 1)
            for c in range(2 * R):
                if c >= 2:
                    pe.wait_ge(wt_out, c - 1)
                for k in range(KT):
                    mm = nc.tensor.transpose(psX[c % 2][:, k * P:(k + 1) * P], Wnat[:, c, k * P:(k + 1) * P], ident[:, :])
                mm.then_inc(wt_mm, 1)

            def turn_x(n, b, cond):
                pe.wait_ge(x_in[b], cond)
                pe.wait_ge(sc_out, n - 1)
                for k in range(KT):
                    mm = nc.tensor.transpose(psX[b][:, k * P:(k + 1) * P], xin[:, b, k * P:(k + 1) * P], ident[:, :])
                mm.then_inc(xt_mm, 1)

            def score(n, b, cols):
                pe.wait_ge(xt_out, n + 1)
                for k in range(KT):
                    mm = nc.tensor.matmul(psX[b][:, 256:320], xT[:, b, k, :], A[:, k, cols], start=k == 0, stop=k == 1)
                mm.then_inc(sc_mm, 1)

            pe.wait_ge(a_out, 4)
            pe.wait_ge(wt_out, 2 * R)
            pe.wait_ge(tabs, 1)
            dcols, scols = slice(64, 128), slice(0, 64)
            for b in range(2):
                pe.wait_ge(x_in[b], 16)
                for k in range(KT):
                    mm = nc.tensor.transpose(psX[b][:, k * P:(k + 1) * P], xin[:, b, k * P:(k + 1) * P], ident[:, :])
                mm.then_inc(xt_mm, 1)
                pe.wait_ge(xt_out, b + 1)
                for k in range(KT):
                    mm = nc.tensor.matmul(psX[b][:, 256:320], xT[:, b, k, :], A[:, k, dcols], start=k == 0, stop=k == 1)
                mm.then_inc(sc_mm, 1)
            with pe.Fori(1, SWEEPS) as i:
                for b in range(2):
                    turn_x(i * 2 + b, b, i * 16 + 16)
                    score(i * 2 + b, b, dcols)
            n = WINDOWS - 1
            turn_x(n, 0, 16 * (SWEEPS + 1))
            score(n, 0, dcols)

            def sd_step(s, c, n):
                pe.wait_ge(sdw_in[pe_slot[0]], n)
                pe.wait_ge(oht, s + 1)
                if c is not None:
                    pe.wait_ge(sdm_made, c)
                b = pe_par[0]
                pe_par[0] ^= 1
                for t in range(T):
                    mm = nc.tensor.matmul(psE[b][0:EP, t * 64:t * 64 + 64],
                                          ohT[:, b, :].rearrange("p (e t) -> p t e", t=T)[:, t, :],
                                          sdw[:, pe_slot[0], :], start=True, stop=True)
                pe_slot[0] = (pe_slot[0] + 1) % PRE
                mm.then_inc(sd_mm, 1)

            pe_par, pe_slot = [0], [0]

            def table_tile(i, n, b, xcond, steps, hcond, first):
                turn_x(n, b, xcond)
                score(n, b, scols)
                for c in range(4):
                    if hcond is not None:
                        pe.wait_ge(h_out, hcond + c)
                    for k in range(KT):
                        mm = nc.tensor.matmul(psH[c][:, :], xT[:, b, k, :], WT[:, k, c * 512:c * 512 + 512], start=k == 0, stop=k == 1)
                    mm.then_inc(h_mm, 1)
                for j in range(steps):
                    sd_step(i * PRE + j, None if first and j < 2 else i * PRE + j - 1, i * 16 + 16)

            table_tile(0, WINDOWS, 1, 16 * (SWEEPS + 1), PRE, None, True)
            table_tile(1, WINDOWS + 1, 0, 16 * (SWEEPS + 2), PRE, 1, False)
            with pe.Fori(1, SWEEPS) as i:
                for b in range(2):
                    table_tile(i * 2 + b, i * 2 + b + WINDOWS, 1 - b, (i + SWEEPS + 1 + b) * 16, PRE, (i * 2 + b - 1) * 4 + 1, False)
            n = WINDOWS - 1
            table_tile(n, WINDOWS + n, 1, 16 * (2 * SWEEPS + 1), PRE - 1, (n - 1) * 4 + 1, False)

            def sums(q, g):
                s = q * Q + g
                pe.wait_ge(oh_made, s + 1)
                pe.wait_ge(msg_made, s + 1)
                pe.wait_ge(first_made, q + 1)
                pe.wait_ge(acc_made, s + 1)
                for t in range(T):
                    mm = nc.tensor.matmul(psP[g % 2][:, 0:GROW], onehot[:, g % 2, t, :], G[:, slot[0], g * T + t, :],
                                          start=t == 0, stop=t == T - 1)
                mm.then_inc(p_mm, 1)

            def turn_scores(q):
                pe.wait_ge(s4_made, q + 1)
                if not isinstance(q, int):
                    pe.wait_ge(sT_out, q)
                for t in range(T):
                    mm = nc.tensor.transpose(psT[:, t * P:t * P + EP], s4[:, t, :, :].rearrange("p g h -> p (g h)"), ident[0:EP, 0:EP])
                mm.then_inc(sT_mm, 1)

            def turn_max(q):
                pe.wait_ge(mT_made, q + 1)
                if not isinstance(q, int):
                    pe.wait_ge(first_made, q)
                for t in range(T):
                    mm = nc.tensor.transpose(psM[0:EP, t * P:(t + 1) * P], mT[:, :].rearrange("p (e t) -> p t e", t=T)[:, t, :], ident[:, :])
                mm.then_inc(m_mm, 1)

            slot = [0]
            pe.wait_ge(h_out, 4 * WINDOWS)
            turn_scores(0)
            turn_max(0)
            with pe.Fori(0, (QUADS - 1) // SLOTS) as i:
                for z in range(SLOTS):
                    q = i * SLOTS + z + 1
                    slot[0] = z
                    sums(q - 1, 0)
                    turn_scores(q)
                    sums(q - 1, 1)
                    turn_max(q)
                    sums(q - 1, 2)
                    sums(q - 1, 3)
            slot[0] = (QUADS - 1) % SLOTS
            for g in range(Q):
                sums(QUADS - 1, g)

        @block.scalar
        def _(act):
            def load_x(n_tile, b, rows=P):
                act.dma_start(xin[0:rows, b, :], x[ds(n_tile * P, rows), :]).then_inc(x_in[b], 16)

            for a, v in enumerate((attn_src, attn_dst)):
                act.dma_start(attn_col[:, a, :], v.rearrange("h d -> (h d)").rearrange("(a o) -> o a", a=2), allow_slow_non_contiguous=True).then_inc(attn_in, 16)
            load_x(0, 0)
            load_x(1, 1)
            act.wait_ge(a_mm, 1)
            pa = psD[:, 0:256].rearrange("p (k r c) -> p k r c", k=KT, r=R)
            for k in range(KT):
                nc.scalar.copy(A[:, k, 0:64].rearrange("p (r h) -> p r h", r=R), pa[:, k, :, 0:H]).then_inc(a_out, 1)
                nc.scalar.copy(A[:, k, 64:128].rearrange("p (h r) -> p r h", r=R), pa[:, k, :, H:2 * H]).then_inc(a_out, 1)
            for c in range(2 * R):
                act.wait_ge(wt_mm, c + 1)
                nc.scalar.copy(WT[:, :, c * P:(c + 1) * P], psX[c % 2][:, 0:256].rearrange("p (k n) -> p k n", k=KT)).then_inc(wt_out, 1)

            def keep_xT(n, b, cond):
                act.wait_ge(xt_mm, n + 1)
                if cond is not None:
                    cond(n)
                nc.scalar.copy(xT[:, b, :, :], psX[b][:, 0:256].rearrange("p (k n) -> p k n", k=KT)).then_inc(xt_out, 1)

            def keep_sdst(n, b, stored):
                act.wait_ge(sc_mm, n + 1)
                if stored is not None:
                    act.wait_ge(sd_st[b], stored)
                nc.scalar.copy(sdo[:, b, :], psX[b][:, 256:320]).then_inc(sc_out, 1)
                act.wait_ge(sc_out, n + 1)
                act.dma_start(sdst_d[ds(n, 1), :, :].rearrange("a p c -> p (a c)"), sdo[:, b, :]).then_inc(sd_st[b], 16)

            for b in range(2):
                keep_xT(b, b, None)
                load_x(b + 2, b)
                keep_sdst(b, b, None)
            with act.Fori(1, SWEEPS - 1) as i:
                for b in range(2):
                    keep_xT(i * 2 + b, b, lambda n: act.wait_ge(sc_mm, n - 1))
                    load_x(i * 2 + b + 2, b)
                    keep_sdst(i * 2 + b, b, i * 16)
            n = WINDOWS - 3
            keep_xT(n, 0, lambda n: act.wait_ge(sc_mm, n - 1))
            load_x(WINDOWS - 1, 0, TAIL)
            keep_sdst(n, 0, 16 * (SWEEPS - 1))
            keep_xT(n + 1, 1, lambda n: act.wait_ge(sc_mm, n - 1))
            load_x(0, 1)
            keep_sdst(n + 1, 1, 16 * (SWEEPS - 1))
            keep_xT(n + 2, 0, lambda n: act.wait_ge(sc_mm, n - 1))
            load_x(1, 0)
            keep_sdst(n + 2, 0, 16 * SWEEPS)

            def keep_tile(i, n, b, hb, stored, load, hmm, rows=P):
                act.wait_ge(xt_mm, n + 1)
                act.wait_ge(sc_mm, n - 1)
                if hmm is not None:
                    act.wait_ge(h_mm, hmm)
                nc.scalar.copy(xT[:, b, :, :], psX[b][:, 0:256].rearrange("p (k n) -> p k n", k=KT)).then_inc(xt_out, 1)
                if load is not None:
                    load_x(*load)
                act.wait_ge(sc_mm, n + 1)
                if stored is not None:
                    act.wait_ge(h_st[hb], stored)
                nc.scalar.copy(hbuf[:, hb, :, F:ROW], psX[b][:, 256:320].rearrange("p (r h) -> p r h", r=R)).then_inc(sc_out, 1)
                for c in range(4):
                    act.wait_ge(h_mm, i * 4 + c + 1)
                    nc.scalar.copy(hbuf[:, hb, 2 * c:2 * c + 2, 0:F], psH[c][:, :].rearrange("p (r n) -> p r n", r=2)).then_inc(h_out, 1)
                act.wait_ge(h_out, i * 4 + 4)
                act.wait_ge(sc_out, n + 1)
                act.dma_start(table[ds(i * P * R, rows * R), :].rearrange("(p r) c -> p (r c)", r=R),
                              hbuf[0:rows, hb, :, :].rearrange("p r c -> p (r c)")).then_inc(h_st[hb], 16)

            for b in range(2):
                keep_tile(b, WINDOWS + b, 1 - b, b, None, (b + 2, 1 - b), None)
            with act.Fori(1, SWEEPS - 1) as i:
                for b in range(2):
                    t_ = i * 2 + b
                    keep_tile(t_, t_ + WINDOWS, 1 - b, b, i * 16, (t_ + 2, 1 - b), (t_ - 1) * 4)
            n = WINDOWS - 3
            keep_tile(n, WINDOWS + n, 1, 0, 16 * (SWEEPS - 1), (WINDOWS - 1, 1, TAIL), (n - 1) * 4)
            keep_tile(n + 1, WINDOWS + n + 1, 0, 1, 16 * (SWEEPS - 1), None, n * 4)
            keep_tile(n + 2, WINDOWS + n + 2, 1, 0, 16 * SWEEPS, None, (n + 1) * 4, TAIL)

            def keep_sT(q):
                act.wait_ge(sT_mm, q + 1)
                if not isinstance(q, int):
                    act.wait_ge(fwd_made, q)
                nc.scalar.activation(sT[:, :].rearrange("p (e t) -> p e t", t=T),
                                     psT[:, :].rearrange("p (t e) -> p e t", t=T)[:, 0:EP, :], ACT.Relu).then_inc(sT_out, 1)

            def weights(q, z):
                act.wait_ge(dif_made, q + 1)
                nc.scalar.activation(G[:, z, :, F:ROW].rearrange("p (g t) h -> p g t h", g=Q),
                                     dif[:, :, :].rearrange("p (t g) h -> p g t h", g=Q), ACT.Exp).then_inc(w_made, 1)

            def shifts(q, g):
                s = q * Q + g
                act.wait_ge(dab_made, s * 2 + 2)
                act.wait_ge(acc_made, s + 2)
                nc.scalar.activation(eab[:, :], dab[:, :], ACT.Exp).then_inc(eab_made, 1)

            keep_sT(0)
            weights(0, 0)
            with act.Fori(0, (QUADS - 1) // SLOTS) as i:
                for z in range(SLOTS):
                    q = i * SLOTS + z + 1
                    keep_sT(q)
                    shifts(q - 1, 0)
                    shifts(q - 1, 1)
                    shifts(q - 1, 2)
                    weights(q, (z + 1) % SLOTS)
                    shifts(q - 1, 3)
            for g in range(Q):
                shifts(QUADS - 1, g)

            def root(w, b):
                act.wait_ge(mv_made, w + 1)
                nc.scalar.activation(sd_[:, b, :], mv[:, b, 1:2], ACT.Sqrt, bias=eps[:, 0:1]).then_inc(root_made, 1)
            with act.Fori(0, SWEEPS) as i:
                for b in range(2):
                    root(i * 2 + b, b)
            root(WINDOWS - 1, 0)

        @block.vector
        def _(dve):
            v = nc.vector
            v.memset(s4[:, :, :, :], 0.0).then_inc(zeroed, 1)
            v.memset(brk[:, :, :, :], 0.0).then_inc(zeroed, 1)
            v.memset(accS[:, :, :], 0.0).then_inc(acc_made, 2)
            v.memset(M[:, :, :], 0.0).then_inc(mnew, 1)
            v.memset(eps[:, :], LN_EPS).then_inc(zeroed, 1)
            v.memset(keep[:, 0:1], 0.0).then_inc(zeroed, 1)
            dve.wait_ge(attn_in, 32)
            dve.wait_ge(consts, 5)
            for a in range(2):
                v.tensor_tensor(Bd[:, :, a * H:(a + 1) * H], headsel[:, :, :],
                                attn_col[:, a, :].unsqueeze(2).to_broadcast([P, 2, H]), ALU.mult).then_inc(bd_made, 1)
            v.tensor_copy(pcol[:, :], iota_col[:, :]).then_inc(pcol_made, 1)
            dve.wait_ge(edges_in, 48)
            v.memset(recE[:, 0:1, 3:4], 1).then_inc(prep, 1)
            v.memset(brkE[:, 0, 0:1], -BIG).then_inc(prep, 1)
            v.memset(brkE[:, 1, GE - 1:GE], -BIG).then_inc(prep, 1)
            v.tensor_tensor(neE[:, 1:GE], dstE[:, 1:GE], dstE[:, 0:GE - 1], ALU.not_equal).then_inc(ne_made, 1)
            v.tensor_scalar(wlast[:, :], dstE[:, GE - 1:GE], 7, None, ALU.arith_shift_right).then_inc(last_made, 1)
            v.scalar_tensor_tensor(out=recE[:, :, 0], in0=srcE[:, :], scalar=float(R), in1=typE[:, :], op0=ALU.mult, op1=ALU.add).then_inc(cols_made, 1)
            v.tensor_copy(recE[:, :, 1], dstE[:, :]).then_inc(cols_made, 1)
            v.tensor_copy(recE[:, :, 2], typE[:, :]).then_inc(cols_made, 1)
            dve.wait_ge(cols_made, 3)
            v.tensor_copy(dstF[:, :], dstE[:, :]).then_inc(prep, 1)
            dve.wait_ge(ne_made, 1)
            v.tensor_copy(recE[:, 1:GE, 3], neE[:, 1:GE]).then_inc(prep, 1)
            v.tensor_scalar(brkE[:, 0, 1:GE], neE[:, 1:GE], -BIG, None, ALU.mult).then_inc(prep, 1)
            v.tensor_scalar(brkE[:, 1, 0:GE - 1], neE[:, 1:GE], -BIG, None, ALU.mult).then_inc(prep, 1)
            dve.wait_ge(last_made, 1)
            v.tensor_copy(wlastF[:, :], wlast[:, :]).then_inc(last_made, 1)
            v.tensor_tensor(glast[:, :], wlast[:, :], iota_col[0:GROUPS, :], ALU.add).then_inc(last_made, 1)
            dve.wait_ge(last_made, 3)
            dve.wait_ge(pcol_made, 1)
            v.tensor_scalar(cmp[:, 0:STEPS], iota_row[0:GROUPS, 0:STEPS], glast[:, 0:1], None, ALU.is_gt).then_inc(cmp_made, 1)
            v.tensor_scalar(cmp[:, STEPS:STEPS + WINDOWS], iota_row[0:GROUPS, 0:WINDOWS], wlastF[:, 0:1], None, ALU.is_ge).then_inc(cmp_made, 1)
            dve.wait_ge(cnt_mm, 1)
            v.tensor_scalar(cnt[:, :], psS[:, 0:STEPS + WINDOWS], float(GROUPS - 1), None, ALU.min).then_inc(tabs, 1)
            dve.wait_ge(tabs, 1)
            v.tensor_tensor(win[:, :], iota_row[:, 0:STEPS], cnt[:, 0:STEPS], ALU.subtract).then_inc(win_made, 1)
            v.tensor_copy(gtab[:, :], cnt[0:1, 0:STEPS]).then_inc(tabs, 1)
            v.tensor_tensor(ltab[:, :], cnt[0:1, STEPS:STEPS + WINDOWS], iota_row[0:1, 0:WINDOWS], ALU.add).then_inc(tabs, 1)
            dve.wait_ge(win_made, 1)
            v.tensor_copy(wtab[:, :], win[0:1, :]).then_inc(tabs, 1)
            v.tensor_scalar(node[:, :], win[:, :], float(P), pcol[:, 0:1], ALU.mult, ALU.add).then_inc(tabs, 1)
            v.tensor_scalar(win128[:, :], win[:, :], float(P), None, ALU.mult).then_inc(tabs, 1)
            v.tensor_tensor(keep[:, 1:STEPS], win[:, 1:STEPS], win[:, 0:STEPS - 1], ALU.is_equal).then_inc(tabs, 1)
            dve.wait_ge(tabs, 7)
            dve.wait_ge(zeroed, 4)

            def oht_step(s, j, b, n, cond):
                dve.wait_ge(drow_in[j], n)
                dve.wait_ge(rec_in[j], n)
                if cond is not None:
                    dve.wait_ge(sd_mm, cond)
                v.tensor_scalar(ohT[:, b, :], drow[:, j, :], node[:, ds(s, 1)], None, ALU.is_equal).then_inc(oht, 1)
                v.tensor_tensor(rmask[:, b, :, :], rec[:, ds(s, 1), :, 2:3].rearrange("p a t c -> p (a t) c").to_broadcast([EP, T, R]),
                                iota_row[0:EP, 0:R].unsqueeze(1).to_broadcast([EP, T, R]), ALU.is_equal).then_inc(rm_made, 1)

            def pick_step(s, b):
                dve.wait_ge(sd_mm, s + 1)
                dve.wait_ge(rm_made, s + 1)
                v.tensor_tensor(sdm[:, b, :, :].rearrange("p (t h) r -> p t h r", t=T),
                                psE[b][0:EP, 0:256].rearrange("p (t h r) -> p t h r", t=T, h=H),
                                rmask[:, b, :, :].unsqueeze(2).to_broadcast([EP, T, H, R]), ALU.mult).then_inc(sdm_made, 1)
                dve.wait_ge(sdm_made, s + 1)
                v.tensor_reduce(sdS[:, ds(s, 1), :, :].rearrange("p a t h -> p (a t h)"), sdm[:, b, :, :],
                                axis=AXX, op=ALU.add).then_inc(sd_done, 1)

            oht_step(0, 0, 0, 16, None)
            oht_step(1, 1, 1, 16, None)
            pick_step(0, 0)
            with dve.Fori(0, SWEEPS) as i:
                for j in range(2 * PRE):
                    s = i * (2 * PRE) + j + 2
                    oht_step(s, (j + 2) % PRE, j % 2, (i * 2 + (j + 2) // PRE + 1) * 16, s - 1)
                    pick_step(s - 1, (j + 1) % 2)
            for s in (STEPS - 2, STEPS - 1):
                oht_step(s, s % PRE, s % 2, (s // PRE + 1) * 16, s - 1)
                pick_step(s - 1, (s - 1) % 2)
            pick_step(STEPS - 1, 1)
            dve.wait_ge(sd_done, STEPS)

            def scores(q, z, n):
                for g in range(Q):
                    dve.wait_ge(gath[z][g], n)
                v.tensor_tensor(sraw[:, :, :].rearrange("p (t g) h -> p g t h", g=Q),
                                G[:, z, :, F:ROW].rearrange("p (g t) h -> p g t h", g=Q),
                                sdS[:, ds(q * Q, Q), :, :], ALU.add).then_inc(sraw_made, 1)
                dve.wait_ge(sraw_made, q + 1)
                v.scalar_tensor_tensor(out=s4[:, :, :, 0:H].rearrange("p t g h -> p (t g) h"), in0=sraw[:, :, :],
                                       scalar=NEG_SLOPE, in1=sraw[:, :, :], op0=ALU.mult, op1=ALU.max).then_inc(s4_made, 1)

            def scans(q, b, n):
                dve.wait_ge(sT_out, q + 1)
                dve.wait_ge(brk_in[b], n)
                v.tensor_tensor_scan(fwd[:, :], brk[:, b, 0, :], sT[:, :], -BIG, ALU.add, ALU.max).then_inc(fwd_made, 1)
                dve.wait_ge(fwd_made, q + 1)
                if not isinstance(q, int):
                    dve.wait_ge(m_mm, q)
                v.tensor_tensor_scan(mT[:, ::-1], brk[:, b, 1, ::-1], fwd[:, ::-1], -BIG, ALU.add, ALU.max).then_inc(mT_made, 1)

            def shifted(q, z):
                dve.wait_ge(m_mm, q + 1)
                pm = psM[0:EP, :].rearrange("p (c h) -> p c h", h=PAD)[:, :, 0:H]
                if not isinstance(q, int):
                    dve.wait_ge(w_made, q)
                v.tensor_tensor(dif[:, :, :], s4[:, :, :, 0:H].rearrange("p t g h -> p (t g) h"), pm, ALU.subtract).then_inc(dif_made, 1)
                v.tensor_tensor(G[:, z, :, ROW:GROW].rearrange("p (g t) h -> p g t h", g=Q),
                                pm.rearrange("p (t g) h -> p g t h", g=Q),
                                rec[:, ds(q * Q, Q), :, 3:4].to_broadcast([EP, Q, T, H]), ALU.mult).then_inc(first_made, 1)

            def messages(q, z, g):
                s = q * Q + g
                v.scalar_tensor_tensor(out=onehot[:, g % 2, :, :],
                                       in0=rec[:, ds(s, 1), :, 1:2].rearrange("p a t c -> p (a t) c").to_broadcast([EP, T, P]),
                                       scalar=win128[0:EP, ds(s, 1)],
                                       in1=iota_row[0:EP, :].unsqueeze(1).to_broadcast([EP, T, P]),
                                       op0=ALU.subtract, op1=ALU.is_equal).then_inc(oh_made, 1)
                dve.wait_ge(w_made, q + 1)
                f = G[:, z, g * T:(g + 1) * T, 0:F].rearrange("p t (h d) -> p t h d", h=H)
                v.tensor_tensor(f, f, G[:, z, g * T:(g + 1) * T, F:ROW].unsqueeze(3).to_broadcast([EP, T, H, D]), ALU.mult).then_inc(msg_made, 1)

            def merge(q, g):
                s = q * Q + g
                b, o_ = g % 2, (g + 1) % 2
                dve.wait_ge(p_mm, s + 1)
                k = keep[:, ds(s, 1)]
                pp = psP[b]
                dve.wait_ge(mnew, s + 1)
                v.scalar_tensor_tensor(out=M[:, b, :], in0=M[:, o_, :], scalar=k, in1=pp[:, ROW:GROW], op0=ALU.mult, op1=ALU.max).then_inc(mnew, 1)
                dve.wait_ge(mnew, s + 2)
                v.scalar_tensor_tensor(out=dab[:, 0:H], in0=M[:, o_, :], scalar=k, in1=M[:, b, :], op0=ALU.mult, op1=ALU.subtract).then_inc(dab_made, 1)
                v.tensor_tensor(dab[:, H:2 * H], pp[:, ROW:GROW], M[:, b, :], ALU.subtract).then_inc(dab_made, 1)
                dve.wait_ge(eab_made, s + 1)
                dve.wait_ge(acc_made, s + 2)
                ea = eab[:, 0:H]
                eb = eab[:, H:2 * H]
                dve.wait_ge(acc_st[b], (s - b) * 8 + 16)
                for lo, hi, d in ((0, F, D), (F, ROW, 1)):
                    v.scalar_tensor_tensor(out=accS[:, b, lo:hi].rearrange("p (h d) -> p h d", h=H),
                                           in0=accS[:, o_, lo:hi].rearrange("p (h d) -> p h d", h=H), scalar=k,
                                           in1=ea.unsqueeze(2).to_broadcast([P, H, d]), op0=ALU.mult, op1=ALU.mult).then_inc(t1, 1)
                    i_ = v.tensor_tensor(tsum[:, lo:hi].rearrange("p (h d) -> p h d", h=H),
                                         pp[:, lo:hi].rearrange("p (h d) -> p h d", h=H),
                                         eb.unsqueeze(2).to_broadcast([P, H, d]), ALU.mult)
                i_.then_inc(t2, 1)
                dve.wait_ge(t1, s * 2 + 2)
                dve.wait_ge(t2, s + 1)
                v.tensor_tensor(accS[:, b, :], accS[:, b, :], tsum[:, :], ALU.add).then_inc(acc_made, 1)

            scores(0, 0, 16 * T)
            scans(0, 0, 16 * Q)
            shifted(0, 0)
            with dve.Fori(0, (QUADS - 1) // (2 * SLOTS)) as i:
                for c in range(2 * SLOTS):
                    q = i * (2 * SLOTS) + c + 1
                    zq, zp = (c + 1) % SLOTS, c % SLOTS
                    messages(q - 1, zp, 0)
                    scores(q, zq, (i * 2 + (c + 1) // SLOTS + 1) * 16 * T)
                    messages(q - 1, zp, 1)
                    merge(q - 1, 0)
                    scans(q, (c + 1) % 2, (i * SLOTS + (c + 1) // 2 + 1) * 16 * Q)
                    messages(q - 1, zp, 2)
                    merge(q - 1, 1)
                    messages(q - 1, zp, 3)
                    merge(q - 1, 2)
                    shifted(q, zq)
                    merge(q - 1, 3)
            zl = (QUADS - 1) % SLOTS
            messages(QUADS - 1, zl, 0)
            for g in range(1, Q):
                messages(QUADS - 1, zl, g)
                merge(QUADS - 1, g - 1)
            merge(QUADS - 1, Q - 1)

            def finish(w, b, n, ocond):
                dve.wait_ge(fin_in[b], n)
                v.tensor_scalar(rden[:, b, :], fin[:, b, F:ROW], DENOM_EPS, None, ALU.add).then_inc(mean_made, 1)
                dve.wait_ge(mean_made, w * 4 + 1)
                v.reciprocal(rden[:, b, :], rden[:, b, :]).then_inc(mean_made, 1)
                dve.wait_ge(mean_made, w * 4 + 2)
                v.tensor_tensor(y[:, b, :].rearrange("p (h d) -> p h d", h=H), fin[:, b, 0:F].rearrange("p (h d) -> p h d", h=H),
                                rden[:, b, :].unsqueeze(2).to_broadcast([P, H, D]), ALU.mult).then_inc(mean_made, 1)
                dve.wait_ge(mean_made, w * 4 + 3)
                v.tensor_tensor(y[:, b, :], y[:, b, :], xres[:, b, :], ALU.add).then_inc(mean_made, 1)
                dve.wait_ge(mean_made, w * 4 + 4)
                v.bn_stats(st[:, b, :], y[:, b, :]).then_inc(stats_made, 1)
                dve.wait_ge(stats_made, w + 1)
                dve.nop(nofuse=True)
                v.bn_aggr(mv[:, b, :], st[:, b, :]).then_inc(mv_made, 1)
                dve.wait_ge(root_made, w + 1)
                v.reciprocal(sd_[:, b, :], sd_[:, b, :]).then_inc(rstd_made, 1)
                dve.wait_ge(rstd_made, w + 1)
                if ocond is not None:
                    dve.wait_ge(o_st[b], ocond)
                v.tensor_scalar(o[:, b, :], y[:, b, :], mv[:, b, 0:1], sd_[:, b, 0:1], ALU.subtract, ALU.mult).then_inc(o_made, 1)

            finish(0, 0, 32, None)
            finish(1, 1, 32, None)
            with dve.Fori(1, SWEEPS) as i:
                for b in range(2):
                    finish(i * 2 + b, b, i * 32 + 32, i * 16)
            finish(WINDOWS - 1, 0, 32 * (SWEEPS + 1), 16 * SWEEPS)


def kernel(x, src, dst, edge_type_8, L0_gnn_W, L0_gnn_attn_src, L0_gnn_attn_dst):
    import concourse.bacc as bacc
    from concourse import mybir
    from concourse.bass_utils import run_bass_kernel_spmd

    nc = bacc.Bacc("TRN2", target_bir_lowering=False, num_devices=1)
    named = {"x": x, "src": src, "dst": dst, "etype": edge_type_8, "W": L0_gnn_W,
             "attn_src": L0_gnn_attn_src, "attn_dst": L0_gnn_attn_dst}
    arrays, aps = {}, {}
    for name, a in named.items():
        a = np.ascontiguousarray(a)
        arrays[f"in_{name}"] = a
        aps[name] = nc.dram_tensor(f"in_{name}", a.shape, mybir.dt.from_np(a.dtype), kind="ExternalInput").ap()
    out = nc.dram_tensor("out_0", (N, F), mybir.dt.float32, kind="ExternalOutput").ap()
    gnn_kernel(nc, out=out, **aps)
    r = run_bass_kernel_spmd(nc, [arrays], core_ids=[0])
    return r.results[0]["out_0"]
```

```python
import numpy as np

N, F = 3125, 256
R, H, D = 8, 8, 32
E = 50000
NEG_SLOPE = 0.2
DENOM_EPS = 1e-12
LN_EPS = 1e-5

P = 128
KT = F // P
WINDOWS = -(-N // P)
TAIL = N - (WINDOWS - 1) * P
EP = 125
T = 4
GE = EP * T
GROUPS = E // GE
STEPS = GROUPS - 1 + WINDOWS
Q = 4
QUADS = STEPS // Q
SLOTS = 3
ROW = F + H
HD = D + 1
GROW = ROW + H
C = 4
PRE = 5
PAD = 32
BIG = 1e30
assert GROUPS * GE == E and QUADS * Q == STEPS and PRE * WINDOWS == STEPS + 1
assert (QUADS - 1) % SLOTS == 0 and WINDOWS % (2 * C) == 1


def gnn_kernel(nc, x, src, dst, etype, W, attn_src, attn_dst, out):
    import concourse.bass as bass
    from concourse import mybir
    from contextlib import ExitStack

    ALU = mybir.AluOpType
    ACT = mybir.ActivationFunctionType
    F32 = mybir.dt.float32
    F32R = mybir.dt.float32r
    BF16 = mybir.dt.bfloat16
    I32 = mybir.dt.int32
    I16 = mybir.dt.int16
    AXX = mybir.AxisListType.X
    ds = bass.ds

    with ExitStack() as ctx:
        def sb(name, shape, dt=F32, c=ctx):
            return c.enter_context(nc.sbuf_tensor(name, shape, dt))

        def ps(name):
            return ctx.enter_context(nc.psum_tensor(name, [P, 512], F32))

        def sem(name):
            return ctx.enter_context(nc.semaphore(name))

        def dram(name, shape, dt=F32):
            return nc.dram_tensor(name, shape, dt, kind="Internal").ap()

        table = dram("table", [N * R, ROW])
        rec_d = dram("rec_d", [GROUPS, EP, T * 4], I32)
        brk_d = dram("brk_d", [GROUPS, 2 * GE])
        recs_d = dram("recs_d", [STEPS, EP, T * 4], I32)
        brks_d = dram("brks_d", [STEPS, 2 * GE])
        dstrows_d = dram("dstrows_d", [STEPS, GE], I16)
        dstrow_d = dram("dstrow_d", [GROUPS, GE], I16)
        xT_d = dram("xT_d", [WINDOWS, P, 2 * KT * P])
        sdst_d = dram("sdst_d", [WINDOWS, P, 3 * H * R], BF16)

        ident = sb("ident", [P, P])
        iota_row = sb("iota_row", [P, P], I32)
        iota_col = sb("iota_col", [P, 1], I32)
        pcol = sb("pcol", [P, 1])
        cnt = sb("cnt", [P, STEPS])
        win = sb("win", [P, STEPS])
        win128 = sb("win128", [P, STEPS])
        node = sb("node", [P, STEPS])
        keep = sb("keep", [P, STEPS])
        wtab = sb("wtab", [1, STEPS], I32)
        rec = sb("rec", [EP, STEPS, T, 4], I32)
        sdS = sb("sdS", [EP, STEPS, T, H])
        eps = sb("eps", [P, 1])

        build = ExitStack()
        ones = sb("ones", [P, P], c=build)
        headsel = sb("headsel", [P, 2, H], c=build)
        attn_col = sb("attn_col", [P, 2, 2], c=build)
        Bd = sb("Bd", [P, 2, 2 * H], c=build)
        Wnat = sb("Wnat", [P, 2 * R, F], c=build)
        WT = [sb(f"WT{l}", [P, KT, R * F], F32R, build) for l in "hl"]
        A = [sb(f"A{l}", [P, KT, 2 * H * R], F32R, build) for l in "hl"]
        dstE = sb("dstE", [GROUPS, GE], I32, build)
        srcE = sb("srcE", [GROUPS, GE], I32, build)
        typE = sb("typE", [GROUPS, GE], I32, build)
        recE = sb("recE", [GROUPS, GE, 4], I32, build)
        neE = sb("neE", [GROUPS, GE], c=build)
        brkE = sb("brkE", [GROUPS, 2, GE], c=build)
        dst16 = sb("dst16", [GROUPS, GE], I16, build)
        gcol = sb("gcol", [STEPS, 1], I32, build)
        recS = sb("recS", [STEPS, EP * T * 4], I32, build)
        brkS = sb("brkS", [STEPS, 2 * GE], c=build)
        dstS = sb("dstS", [STEPS, GE], I16, build)
        wlast = sb("wlast", [GROUPS, 1], I32, build)
        glast = sb("glast", [GROUPS, 1], c=build)
        cmp = sb("cmp", [GROUPS, STEPS], c=build)
        xin = sb("xin", [P, 2, C, F], c=build)
        xTs = sb("xTs", [P, 2, C, 2, KT * P], F32R, build)
        sdo = sb("sdo", [P, 2, C, 3, H * R], BF16, build)
        sdr = sb("sdr", [P, 2, H * R], c=build)
        ssrc = sb("ssrc", [P, WINDOWS, R * H], c=build)
        xT = sb("xT", [P, 2, 2, KT, P], F32R, build)
        hbuf = sb("hbuf", [P, 2, R, H, HD], c=build)
        drow = sb("drow", [P, PRE, GE], I16, build)
        sdw = sb("sdw", [P, PRE, 3, H * R], BF16, build)
        ohT = sb("ohT", [P, 2, GE], BF16, build)
        rmask = sb("rmask", [EP, 2, T, R], c=build)
        sdm = sb("sdm", [EP, 2, T * H, R], c=build)
        build.close()

        G = sb("G", [EP, SLOTS, Q * T, GROW])
        idx = sb("idx", [EP, SLOTS, Q * T], I32)
        sraw = sb("sraw", [EP, T * Q, H])
        s4 = sb("s4", [EP, T, Q, PAD])
        sT = sb("sT", [P, GE])
        fwd = sb("fwd", [P, GE])
        mT = sb("mT", [P, GE])
        brk = sb("brk", [P, 2, 2, GE])
        dif = sb("dif", [EP, T * Q, H])
        onehot = sb("onehot", [EP, 2, T, P])
        M = sb("M", [P, 2, H])
        dab = sb("dab", [P, 2, 2 * H])
        eab = sb("eab", [P, 2, 2 * H])
        accS = sb("accS", [P, 2, ROW])
        tsum = sb("tsum", [P, 2, ROW])
        accW = sb("accW", [P, WINDOWS, H, HD])
        xres = sb("xres", [P, WINDOWS, F])
        rden = sb("rden", [P, PRE, H])
        st = sb("st", [P, PRE, 6])
        mv = sb("mv", [P, PRE, 2])
        rstd = sb("rstd", [P, PRE])

        psX = [ps(f"psX{b}") for b in range(2)]
        psH = [ps(f"psH{b}") for b in range(4)]
        psE = [ps(f"psE{b}") for b in range(2)]
        psT, psM = psX
        psP = psH

        edges_in, w_in, attn_in = sem("edges_in"), sem("w_in"), sem("attn_in")
        consts0, consts = sem("consts0"), sem("consts")
        prep, rec_out, tabs = sem("prep"), sem("rec_out"), sem("tabs")
        ne_made, last_made, cols_made = sem("ne_made"), sem("last_made"), sem("cols_made")
        cmp_made, win_made, keep_made, cnt_mm = sem("cmp_made"), sem("win_made"), sem("keep_made"), sem("cnt_mm")
        bd_made, a_mm, a_hi, a_lo = sem("bd_made"), sem("a_mm"), sem("a_hi"), sem("a_lo")
        wt_mm, wt_hi, wt_lo = sem("wt_mm"), sem("wt_hi"), sem("wt_lo")
        x_in = [sem(f"x_in{b}") for b in range(2)]
        xt_mm, xt_hi, xt_lo = sem("xt_mm"), sem("xt_hi"), sem("xt_lo")
        sc_mm, ssrc_out, sd_hi, sd_lo = sem("sc_mm"), sem("ssrc_out"), sem("sd_hi"), sem("sd_lo")
        chunk_st = [sem(f"chunk_st{b}") for b in range(2)]
        xT_in = [sem(f"xT_in{b}") for b in range(2)]
        h_mm, h_out, hs_out = sem("h_mm"), sem("h_out"), sem("hs_out")
        h_st = [sem(f"h_st{b}") for b in range(2)]
        drow_in = [sem(f"drow_in{b}") for b in range(PRE)]
        sdw_in = [sem(f"sdw_in{b}") for b in range(PRE)]
        sd_parts = sem("sd_parts")
        rec_in, gcol_made, steps_in = sem("rec_in"), sem("gcol_made"), sem("steps_in")
        dsts_out, recs_out, brks_out = sem("dsts_out"), sem("recs_out"), sem("brks_out")
        oht, rm_made, sd_mm, sdm_made, sd_done = sem("oht"), sem("rm_made"), sem("sd_mm"), sem("sdm_made"), sem("sd_done")
        idx_made = sem("idx_made")
        gath = [[sem(f"gath{z}_{g}") for g in range(Q)] for z in range(SLOTS)]
        zeroed, xres_in = sem("zeroed"), sem("xres_in")
        sraw_made, s4_made = sem("sraw_made"), sem("s4_made")
        sT_mm, sT_out = sem("sT_mm"), sem("sT_out")
        brk_in = [sem(f"brk_in{b}") for b in range(2)]
        fwd_made, mT_made, m_mm = sem("fwd_made"), sem("mT_made"), sem("m_mm")
        dif_made, w_made, first_made = sem("dif_made"), sem("w_made"), sem("first_made")
        oh_made, msg_made, p_mm = sem("oh_made"), sem("msg_made"), sem("p_mm")
        mnew, dab_made, eab_made = sem("mnew"), sem("dab_made"), sem("eab_made")
        acc_scaled = sem("acc_scaled")
        scaled, acc_made, acc_st = sem("scaled"), sem("acc_made"), sem("acc_st")
        rd_made, y_made, ysum_made, stats_made = sem("rd_made"), sem("y_made"), sem("ysum_made"), sem("stats_made")
        mv_made, root_made, rstd_made, o_made, o_st = sem("mv_made"), sem("root_made"), sem("rstd_made"), sem("o_made"), sem("o_st")

        block = ctx.enter_context(nc.Block())

        TABS = 4
        SWEEPS = (WINDOWS - 1) // 2
        CHUNKS = (WINDOWS - 1) // C

        @block.sync
        def _(sp):
            sp.dma_start(dstE[:, :], dst.rearrange("(g e) -> g e", g=GROUPS)).then_inc(edges_in, 16)
            for r in range(R):
                sp.dma_start(Wnat[:, 2 * r:2 * r + 2, :], W[r].rearrange("(a o) f -> o a f", a=2)).then_inc(w_in, 16)
            sp.dma_start(srcE[:, :], src.rearrange("(g e) -> g e", g=GROUPS)).then_inc(edges_in, 16)
            sp.dma_start(typE[:, :], etype.rearrange("(g e) -> g e", g=GROUPS)).then_inc(edges_in, 16)
            sp.wait_ge(prep, 7)
            sp.dma_start(rec_d.rearrange("g p c -> g (p c)"), recE[:, :, :].rearrange("g e c -> g (e c)")).then_inc(rec_out, 16)
            sp.dma_start(brk_d, brkE[:, :, :].rearrange("g a e -> g (a e)")).then_inc(rec_out, 16)
            sp.dma_start(dstrow_d, dst16[:, :]).then_inc(rec_out, 16)
            sp.wait_ge(rec_out, 48)
            sp.wait_ge(steps_in, 48)
            sp.dma_start(dstrows_d, dstS[:, :]).then_inc(dsts_out, 16)
            sp.dma_start(recs_d.rearrange("s p c -> s (p c)"), recS[:, :]).then_inc(recs_out, 16)
            sp.dma_start(brks_d, brkS[:, :]).then_inc(brks_out, 16)
            sp.wait_ge(recs_out, 16)
            for k in range(Q):
                ks = slice(k * QUADS, (k + 1) * QUADS)
                sp.dma_start(rec[:, ks, :, :].rearrange("p s t c -> p s (t c)"), recs_d[ks].rearrange("s p c -> p s c")).then_inc(rec_in, 16)

            sp.wait_ge(tabs, TABS)
            for b, n in ((0, CHUNKS // 2 + 1), (1, CHUNKS // 2)):
                sp.wait_ge(chunk_st[b], 32 * n)

            def stage_scores(s, j, cond):
                w = sp.value_load(wtab[0:1, ds(s, 1)], min_val=0, max_val=WINDOWS - 1)
                if cond is not None:
                    sp.wait_ge(sd_mm, cond)
                sp.dma_start(sdw[:, j, :, :].rearrange("p a c -> p (a c)"),
                             sdst_d[ds(w, 1), :, :].rearrange("a p c -> p (a c)")).then_inc(sdw_in[j], 16)

            for j in range(PRE):
                stage_scores(j, j, None)
            with sp.Fori(1, WINDOWS - 1) as i:
                for j in range(PRE):
                    stage_scores(i * PRE + j, j, i * PRE + j + 1 - PRE)
            for j in range(PRE - 1):
                s = (WINDOWS - 1) * PRE + j
                stage_scores(s, j, s + 1 - PRE)
            sp.wait_ge(brks_out, 16)

            def breaks(q, b):
                for g_ in range(Q):
                    sp.dma_start(brk[g_ * PAD:g_ * PAD + H, b, :, :].rearrange("p a e -> p (a e)"),
                                 brks_d[ds(q * Q + g_, 1), :].to_broadcast([H, 2 * GE])).then_inc(brk_in[b], 16)

            def keep_acc(s, b):
                w = sp.value_load(wtab[0:1, ds(s, 1)], min_val=0, max_val=WINDOWS - 1)
                sp.wait_ge(acc_made, s + 3)
                sp.wait_ge(acc_st, s * 16 + 32)
                sp.dma_start(accW[:, ds(w, 1), :, :].rearrange("p a h d -> p (a h d)"), accS[:, b, :]).then_inc(acc_st, 16)

            sp.wait_ge(zeroed, 3)
            sp.wait_ge(acc_made, 2)
            breaks(0, 0)
            breaks(1, 1)
            for b in range(2):
                sp.dma_start(accW[:, b, :, :].rearrange("p h d -> p (h d)"), accS[:, b, :]).then_inc(acc_st, 16)
                sp.wait_ge(acc_st, 16 * (b + 1))
            sp.dma_start(xres[:, 0:WINDOWS - 1, :], x[0:(WINDOWS - 1) * P, :].rearrange("(w p) f -> p w f", p=P)).then_inc(xres_in, 16)
            sp.dma_start(xres[0:TAIL, WINDOWS - 1, :], x[(WINDOWS - 1) * P:N, :]).then_inc(xres_in, 16)
            def quad(q, b):
                for g_ in range(Q):
                    if g_ == 2:
                        sp.wait_ge(mT_made, q - 1)
                        breaks(q, b)
                    keep_acc((q - 2) * Q + g_, g_ % 2)

            quad(2, 0)
            with sp.Fori(1, (QUADS - 1) // 2) as i:
                for b in range(2):
                    quad(i * 2 + b + 1, (b + 1) % 2)
            for s in range((QUADS - 2) * Q, STEPS):
                keep_acc(s, s % 2)

            for c in range(WINDOWS // PRE):
                sp.wait_ge(o_made, PRE * (c + 1))
                whole = PRE if c + 1 < WINDOWS // PRE else PRE - 1
                sp.dma_start(out[c * PRE * P:(c * PRE + whole) * P, :].rearrange("(w p) f -> p w f", p=P),
                             xres[:, c * PRE:c * PRE + whole, :]).then_inc(o_st, 16)
            sp.dma_start(out[(WINDOWS - 1) * P:N, :], xres[0:TAIL, WINDOWS - 1, :]).then_inc(o_st, 16)
            sp.wait_ge(o_st, 16 * (WINDOWS // PRE + 1))

        @block.gpsimd
        def _(pool):
            nc.gpsimd.memset(ident[:, :], 0.0).then_inc(consts0, 1)
            nc.gpsimd.memset(headsel[:, :, :], 1.0).then_inc(consts0, 1)
            nc.gpsimd.iota(iota_row[:, :], pattern=[[1, P]], base=0, channel_multiplier=0).then_inc(consts, 1)
            nc.gpsimd.iota(iota_col[:, :], pattern=[[1, 1]], base=0, channel_multiplier=1).then_inc(consts, 1)
            nc.gpsimd.memset(ones[:, :], 1.0).then_inc(consts, 1)
            pool.wait_ge(consts0, 2)
            nc.gpsimd.affine_select(out=ident[:, :], in_=ident[:, :], compare_op=ALU.not_equal, fill=1.0,
                                    base=0, pattern=[[-1, P]], channel_multiplier=1).then_inc(consts, 1)
            nc.gpsimd.affine_select(out=headsel[:, :, :], in_=headsel[:, :, :], compare_op=ALU.is_ge, fill=0.0,
                                    base=0, pattern=[[P, 2], [-D, H]], channel_multiplier=1).then_inc(consts0, 1)
            pool.wait_ge(consts0, 3)
            nc.gpsimd.affine_select(out=headsel[:, :, :], in_=headsel[:, :, :], compare_op=ALU.is_ge, fill=0.0,
                                    base=D - 1, pattern=[[-P, 2], [D, H]], channel_multiplier=-1).then_inc(consts, 1)

            pool.wait_ge(rec_out, 48)
            pool.wait_ge(gcol_made, 1)
            pool.nop(nofuse=True)
            for rows, table_d in ((dstS, dstrow_d), (recS, rec_d.rearrange("g p c -> g (p c)")), (brkS, brk_d)):
                nc.gpsimd.indirect_dma_start(rows[:, :], None, table_d,
                                             bass.IndirectOffsetOnAxis(ap=gcol[:, 0:1], axis=0)).then_inc(steps_in, 16)

            def stage(s, j, cond):
                if cond is not None:
                    pool.wait_ge(oht, cond)
                pool.dma_start(drow[:, j, :], dstrows_d[ds(s, 1), :].to_broadcast([P, GE])).then_inc(drow_in[j], 16)

            pool.wait_ge(dsts_out, 16)
            for j in range(PRE):
                stage(j, j, None)
            with pool.Fori(1, WINDOWS - 1) as i:
                for j in range(PRE):
                    stage(i * PRE + j, j, i * PRE + j + 1 - PRE)
            for j in range(PRE - 1):
                s = (WINDOWS - 1) * PRE + j
                stage(s, j, s + 1 - PRE)

            pool.wait_ge(rec_in, 16 * Q)
            for b, n in ((0, SWEEPS + 1), (1, SWEEPS)):
                pool.wait_ge(h_st[b], 16 * n)
            pool.wait_ge(sd_done, STEPS)

            def gather(q, z, cond, n=None):
                if n is not None:
                    for g in range(Q):
                        pool.wait_ge(gath[z][g], n)
                nc.gpsimd.tensor_copy(idx[:, z, :].rearrange("p (g t) -> p g t", g=Q),
                                      rec[:, ds(q * Q, Q), :, 0]).then_inc(idx_made, 1)
                pool.wait_ge(idx_made, q + 1)
                pool.nop(nofuse=True)
                for g in range(Q):
                    if cond is not None:
                        pool.wait_ge(p_mm, cond + g)
                        pool.nop(nofuse=True)
                    for t in range(T):
                        nc.gpsimd.indirect_dma_start(G[:, z, g * T + t, 0:ROW], None, table,
                                                     bass.IndirectOffsetOnAxis(ap=idx[:, z, g * T + t:g * T + t + 1], axis=0)).then_inc(gath[z][g], 16)
            for z in range(SLOTS):
                gather(z, z, None)
            with pool.Fori(1, QUADS // SLOTS) as i:
                for z in range(SLOTS):
                    gather(i * SLOTS + z, z, (i * SLOTS + z - SLOTS) * Q + 1, i * 16 * T)
            gather(QUADS - 1, 0, (QUADS - 1 - SLOTS) * Q + 1, (QUADS // SLOTS) * 16 * T)

            pool.wait_ge(xres_in, 32)
            for c in range(WINDOWS // PRE):
                pool.wait_ge(y_made, c + 1)
                cs = slice(c * PRE, (c + 1) * PRE)
                nc.gpsimd.tensor_tensor(xres[:, cs, :].rearrange("p w (h d) -> p (w h) d", h=H), accW[:, cs, :, 0:D].rearrange("p w h d -> p (w h) d"),
                                        xres[:, cs, :].rearrange("p w (h d) -> p (w h) d", h=H), ALU.add).then_inc(ysum_made, 1)

        @block.tensor
        def _(pe):
            HI_LO = ((0, 0), (0, 1), (1, 0))

            pe.wait_ge(consts, 5)
            pe.wait_ge(cmp_made, 1)
            nc.tensor.matmul(psE[0][:, 0:STEPS], ones[0:GROUPS, :], cmp[:, :], start=True, stop=True).then_inc(cnt_mm, 1)
            nc.tensor.matmul(psE[0][0:STEPS, P:P + 1], cmp[:, :], ones[0:GROUPS, 0:1], start=True, stop=True).then_inc(cnt_mm, 1)
            pe.wait_ge(w_in, 16 * R)
            pe.wait_ge(bd_made, 2)
            for r in range(R):
                for k in range(KT):
                    for a in range(2):
                        mm = nc.tensor.matmul(psE[1][:, (k * R + r) * 16:(k * R + r) * 16 + 16],
                                              Wnat[:, 2 * r + a, k * P:(k + 1) * P], Bd[:, a, :], start=a == 0, stop=a == 1)
            mm.then_inc(a_mm, 1)
            pe.wait_ge(a_lo, 4)
            pe.wait_ge(tabs, 1)
            pe.wait_ge(gcol_made, 1)

            def turn_W(c):
                if c >= 4:
                    pe.wait_ge(wt_lo, c - 3)
                for k in range(KT):
                    mm = nc.tensor.transpose(psH[c % 4][:, k * P:(k + 1) * P], Wnat[:, c, k * P:(k + 1) * P], ident[:, :])
                mm.then_inc(wt_mm, 1)

            def turn_x(n, b, cb, j):
                if not (isinstance(n, int) and n < 2):
                    pe.wait_ge(xt_lo, n - 1)
                for k in range(KT):
                    mm = nc.tensor.transpose(psX[b][:, k * P:(k + 1) * P], xin[:, cb, j, k * P:(k + 1) * P], ident[:, :])
                mm.then_inc(xt_mm, 1)

            def score(n, b, cb, j):
                pe.wait_ge(xt_lo, n + 1)
                if not (isinstance(n, int) and n < 2):
                    pe.wait_ge(sd_lo, n - 1)
                    pe.wait_ge(ssrc_out, n - 1)
                for k in range(KT):
                    for m, (xp, ap) in enumerate(HI_LO):
                        mm = nc.tensor.matmul(psE[b][:, 256:384], xTs[:, cb, j, xp, k * P:(k + 1) * P], A[ap][:, k, :],
                                              start=k + m == 0, stop=k == KT - 1 and m == 2)
                mm.then_inc(sc_mm, 1)

            def chunk(c, cb, landed, tiles=C):
                pe.wait_ge(x_in[cb], landed)
                for j in range(tiles):
                    turn_x(c * C + j, j % 2, cb, j)
                    if isinstance(c, int) and c < 2:
                        turn_W((c * C + j) * 2)
                        turn_W((c * C + j) * 2 + 1)
                    if j:
                        score(c * C + j - 1, (j - 1) % 2, cb, j - 1)
                score(c * C + tiles - 1, (tiles - 1) % 2, cb, tiles - 1)

            chunk(0, 0, 16)
            chunk(1, 1, 16)
            with pe.Fori(1, CHUNKS // 2) as i:
                for cb in range(2):
                    chunk(i * 2 + cb, cb, i * 16 + 16)
            chunk(CHUNKS, 0, 16 * (CHUNKS // 2 + 1), 1)

            def sd_step(s, j, b, c, n):
                pe.wait_ge(sdw_in[j], n)
                pe.wait_ge(oht, s + 1)
                if c is not None:
                    pe.wait_ge(sdm_made, c)
                for t in range(T):
                    for m in range(3):
                        mm = nc.tensor.matmul(psE[b][0:EP, t * 64:t * 64 + 64],
                                              ohT[:, b, :].rearrange("p (e t) -> p t e", t=T)[:, t, :],
                                              sdw[:, j, m, :], start=m == 0, stop=m == 2)
                mm.then_inc(sd_mm, 1)

            def table_tile(i, b, landed, steps, hcond, first):
                pe.wait_ge(xT_in[b], landed)
                done = 0
                for c in range(4):
                    if hcond is not None:
                        pe.wait_ge(h_out, hcond + c)
                    for k in range(KT):
                        for m, (xp, wp) in enumerate(HI_LO):
                            mm = nc.tensor.matmul(psH[c][:, :], xT[:, b, xp, k, :], WT[wp][:, k, c * 512:c * 512 + 512],
                                                  start=k + m == 0, stop=k == KT - 1 and m == 2)
                    mm.then_inc(h_mm, 1)
                    for j in range(c, c + 1 + c // 3):
                        if j < steps:
                            sd_step(i * PRE + j, j, (b + j) % 2, None if first and j < 2 else i * PRE + j - 1, i * 16 + 16)

            pe.wait_ge(wt_lo, 2 * R)
            pe.wait_ge(ssrc_out, WINDOWS)
            pe.wait_ge(sd_lo, WINDOWS)
            table_tile(0, 0, 16, PRE, None, True)
            table_tile(1, 1, 16, PRE, 1, False)
            with pe.Fori(1, SWEEPS) as i:
                for b in range(2):
                    table_tile(i * 2 + b, b, i * 16 + 16, PRE, (i * 2 + b - 1) * 4 + 1, False)
            n = WINDOWS - 1
            table_tile(n, 0, 16 * (SWEEPS + 1), PRE - 1, (n - 1) * 4 + 1, False)

            def sums(q, g, z):
                s = q * Q + g
                pe.wait_ge(oh_made, s + 1)
                pe.wait_ge(msg_made, s + 1)
                pe.wait_ge(first_made, q + 1)
                if not (isinstance(q, int) and q == 0):
                    pe.wait_ge(scaled, s - 3)
                for t in range(T):
                    mm = nc.tensor.matmul(psP[g][:, 0:GROW], onehot[:, g % 2, t, :], G[:, z, g * T + t, :],
                                          start=t == 0, stop=t == T - 1)
                mm.then_inc(p_mm, 1)

            def turn_scores(q):
                pe.wait_ge(s4_made, q + 1)
                if not (isinstance(q, int) and q == 0):
                    pe.wait_ge(sT_out, q)
                for t in range(T):
                    mm = nc.tensor.transpose(psT[:, t * P:t * P + EP], s4[:, t, :, :].rearrange("p g h -> p (g h)"), ident[0:EP, 0:EP])
                mm.then_inc(sT_mm, 1)

            def turn_max(q):
                pe.wait_ge(mT_made, q + 1)
                if not (isinstance(q, int) and q == 0):
                    pe.wait_ge(first_made, q)
                for t in range(T):
                    mm = nc.tensor.transpose(psM[0:EP, t * P:(t + 1) * P], mT[:, :].rearrange("p (e t) -> p t e", t=T)[:, t, :], ident[:, :])
                mm.then_inc(m_mm, 1)

            def quad(q, z):
                sums(q - 1, 0, z)
                turn_scores(q)
                sums(q - 1, 1, z)
                turn_max(q)
                sums(q - 1, 2, z)
                sums(q - 1, 3, z)

            pe.wait_ge(h_out, 4 * WINDOWS)
            turn_scores(0)
            turn_max(0)
            for q in range(1, SLOTS + 1):
                quad(q, q - 1)
            with pe.Fori(1, (QUADS - 1) // SLOTS) as i:
                for z in range(SLOTS):
                    quad(i * SLOTS + z + 1, z)
            for g in range(Q):
                sums(QUADS - 1, g, (QUADS - 1) % SLOTS)

        @block.scalar
        def _(act):
            def load_chunk(c, cb):
                act.dma_start(xin[:, cb, :, :], x[ds(c * C * P, C * P), :].rearrange("(j p) f -> p j f", p=P)).then_inc(x_in[cb], 16)

            for a, v in enumerate((attn_src, attn_dst)):
                act.dma_start(attn_col[:, a, :], v.rearrange("h d -> (h d)").rearrange("(a o) -> o a", a=2), allow_slow_non_contiguous=True).then_inc(attn_in, 16)
            load_chunk(0, 0)
            load_chunk(1, 1)
            def keep_W(c):
                act.wait_ge(wt_mm, c + 1)
                nc.scalar.copy(WT[0][:, :, c * P:(c + 1) * P], psH[c % 4][:, 0:256].rearrange("p (k n) -> p k n", k=KT)).then_inc(wt_hi, 1)

            act.wait_ge(a_mm, 1)
            pa = psE[1][:, 0:256].rearrange("p (k r c) -> p k r c", k=KT, r=R)
            for k in range(KT):
                nc.scalar.copy(A[0][:, k, 0:64].rearrange("p (r h) -> p r h", r=R), pa[:, k, :, 0:H]).then_inc(a_hi, 1)
                nc.scalar.copy(A[0][:, k, 64:128].rearrange("p (h r) -> p r h", r=R), pa[:, k, :, H:2 * H]).then_inc(a_hi, 1)

            def keep_xT(n, b, cb, j):
                act.wait_ge(xt_mm, n + 1)
                nc.scalar.copy(xTs[:, cb, j, 0, :], psX[b][:, 0:256]).then_inc(xt_hi, 1)

            def keep_scores(n, b, cb, j):
                act.wait_ge(sc_mm, n + 1)
                nc.scalar.copy(sdo[:, cb, j, 0, :], psE[b][:, 320:384]).then_inc(sd_hi, 1)
                nc.scalar.copy(ssrc[:, ds(n, 1), :].rearrange("p a c -> p (a c)"), psE[b][:, 256:320]).then_inc(ssrc_out, 1)

            def store_chunk(c, cb, tiles=C):
                if tiles == C:
                    act.wait_ge(xt_lo, c * C + C)
                    act.dma_start(xT_d[ds(c * C, C), :, :].rearrange("j p c -> p j c"),
                                  xTs[:, cb, :, :, :].rearrange("p j a c -> p j (a c)").bitcast(F32)).then_inc(chunk_st[cb], 16)
                    act.wait_ge(sd_parts, (c * C + C) * 2)
                    act.dma_start(sdst_d[ds(c * C, C), :, :].rearrange("j p c -> p j c"),
                                  sdo[:, cb, :, :, :].rearrange("p j a c -> p j (a c)")).then_inc(chunk_st[cb], 16)
                else:
                    act.wait_ge(xt_lo, WINDOWS)
                    act.dma_start(xT_d[WINDOWS - 1], xTs[:, cb, 0, :, :].rearrange("p a c -> p (a c)").bitcast(F32)).then_inc(chunk_st[cb], 16)
                    act.wait_ge(sd_parts, 2 * WINDOWS)
                    act.dma_start(sdst_d[WINDOWS - 1], sdo[:, cb, 0, :, :].rearrange("p a c -> p (a c)")).then_inc(chunk_st[cb], 16)

            def keep_chunk(c, cb, stored, load, tiles=C):
                if stored is not None:
                    act.wait_ge(chunk_st[cb], stored)
                for j in range(tiles):
                    keep_xT(c * C + j, j % 2, cb, j)
                    if isinstance(c, int) and c < 2:
                        keep_W((c * C + j) * 2)
                        keep_W((c * C + j) * 2 + 1)
                    if j:
                        keep_scores(c * C + j - 1, (j - 1) % 2, cb, j - 1)
                if load is not None:
                    load()
                keep_scores(c * C + tiles - 1, (tiles - 1) % 2, cb, tiles - 1)
                store_chunk(c, cb, tiles)

            keep_chunk(0, 0, None, lambda: load_chunk(2, 0))
            keep_chunk(1, 1, None, lambda: load_chunk(3, 1))
            with act.Fori(1, CHUNKS // 2 - 1) as i:
                for cb in range(2):
                    keep_chunk(i * 2 + cb, cb, i * 32, lambda: load_chunk(i * 2 + cb + 2, cb))
            keep_chunk(CHUNKS - 2, 0, 32 * (CHUNKS // 2 - 1),
                       lambda: act.dma_start(xin[0:TAIL, 0, 0, :], x[(WINDOWS - 1) * P:N, :]).then_inc(x_in[0], 16))
            keep_chunk(CHUNKS - 1, 1, 32 * (CHUNKS // 2 - 1), None)
            keep_chunk(CHUNKS, 0, 32 * (CHUNKS // 2), None, 1)

            def load_xT(n, b):
                act.dma_start(xT[:, b, :, :, :].rearrange("p a k n -> p (a k n)").bitcast(F32), xT_d[ds(n, 1), :, :].rearrange("a p c -> p (a c)")).then_inc(xT_in[b], 16)

            def keep_tile(i, b, stored, load, rows=P):
                if stored is not None:
                    act.wait_ge(h_st[b], stored)
                nc.scalar.copy(hbuf[:, b, :, :, D], ssrc[:, ds(i, 1), :].rearrange("p a (r h) -> p (a r) h", r=R)).then_inc(hs_out, 1)
                for c in range(4):
                    act.wait_ge(h_mm, i * 4 + c + 1)
                    nc.scalar.copy(hbuf[:, b, 2 * c:2 * c + 2, :, 0:D].rearrange("p r h d -> p (r h) d"),
                                   psH[c][:, :].rearrange("p (r d) -> p r d", d=D)).then_inc(h_out, 1)
                if load is not None:
                    load_xT(i + 2, b)
                act.wait_ge(h_out, i * 4 + 4)
                act.wait_ge(hs_out, i + 1)
                act.dma_start(table[ds(i * P * R, rows * R), :].rearrange("(p r) c -> p (r c)", r=R),
                              hbuf[0:rows, b, :, :, :].rearrange("p r h d -> p (r h d)")).then_inc(h_st[b], 16)

            for b, n in ((0, CHUNKS // 2 + 1), (1, CHUNKS // 2)):
                act.wait_ge(chunk_st[b], 32 * n)
            act.wait_ge(ssrc_out, WINDOWS)
            load_xT(0, 0)
            load_xT(1, 1)
            for b in range(2):
                keep_tile(b, b, None, True)
            with act.Fori(1, SWEEPS - 1) as i:
                for b in range(2):
                    keep_tile(i * 2 + b, b, i * 16, True)
            n = WINDOWS - 3
            keep_tile(n, 0, 16 * (SWEEPS - 1), True)
            keep_tile(n + 1, 1, 16 * (SWEEPS - 1), None)
            keep_tile(n + 2, 0, 16 * SWEEPS, None, TAIL)

            for b, n in ((0, SWEEPS + 1), (1, SWEEPS)):
                act.wait_ge(h_st[b], 16 * n)
            act.wait_ge(sd_done, STEPS)

            def keep_sT(q):
                act.wait_ge(sT_mm, q + 1)
                if not (isinstance(q, int) and q == 0):
                    act.wait_ge(fwd_made, q)
                nc.scalar.activation(sT[:, :].rearrange("p (e t) -> p e t", t=T),
                                     psT[:, :].rearrange("p (t e) -> p e t", t=T)[:, 0:EP, :], ACT.Relu).then_inc(sT_out, 1)

            def weights(q, z):
                act.wait_ge(dif_made, q + 1)
                gw = G[:, z, :, 0:ROW].rearrange("p (g t) (h d) -> p g t h d", g=Q, h=H)
                for g in range(Q):
                    i_ = nc.scalar.activation(gw[:, g, :, :, D],
                                              dif[:, :, :].rearrange("p (t g) h -> p g t h", g=Q)[:, g, :, :], ACT.Exp)
                i_.then_inc(w_made, 1)

            def shifts(q, g):
                s = q * Q + g
                b = g % 2
                act.wait_ge(dab_made, s * 2 + 4)
                act.wait_ge(acc_made, s + 1)
                nc.scalar.activation(eab[:, b, :], dab[:, b, :], ACT.Exp).then_inc(eab_made, 1)
                act.wait_ge(eab_made, s + 1)
                for h in range(H):
                    i_ = nc.scalar.activation(tsum[:, b, h * HD:(h + 1) * HD], psP[g][:, h * HD:(h + 1) * HD], ACT.Copy, scale=eab[:, b, H + h:H + h + 1])
                i_.then_inc(scaled, 1)

            def quad(q, z, before=True):
                if before:
                    shifts(q - 2, 3)
                keep_sT(q)
                shifts(q - 1, 0)
                shifts(q - 1, 1)
                weights(q, (z + 1) % SLOTS)
                shifts(q - 1, 2)

            keep_sT(0)
            weights(0, 0)
            for q in range(1, SLOTS + 1):
                quad(q, q - 1, q > 1)
            with act.Fori(1, (QUADS - 1) // SLOTS) as i:
                for z in range(SLOTS):
                    quad(i * SLOTS + z + 1, z)
            shifts(QUADS - 2, 3)
            for g in range(Q):
                shifts(QUADS - 1, g)

            for c in range(WINDOWS // PRE):
                act.wait_ge(mv_made, PRE * (c + 1))
                nc.scalar.activation(rstd[:, :], mv[:, :, 1], ACT.Sqrt, bias=eps[:, 0:1]).then_inc(root_made, 1)
                act.wait_ge(rstd_made, 2 * (c + 1))
                for j in range(PRE):
                    nc.scalar.activation(xres[:, c * PRE + j, :], xres[:, c * PRE + j, :], ACT.Identity,
                                         bias=mv[:, j, 0:1], scale=rstd[:, j:j + 1]).then_inc(o_made, 1)

        @block.vector
        def _(dve):
            v = nc.vector
            v.memset(eps[:, :], LN_EPS).then_inc(keep_made, 1)
            v.memset(keep[:, 0:1], 0.0).then_inc(keep_made, 1)
            dve.wait_ge(consts, 5)
            v.tensor_copy(pcol[:, :], iota_col[:, :]).then_inc(win_made, 1)
            dve.wait_ge(edges_in, 48)
            v.tensor_scalar(wlast[:, :], dstE[:, GE - 1:GE], 7, None, ALU.arith_shift_right).then_inc(last_made, 1)
            v.tensor_tensor(neE[:, 1:GE], dstE[:, 1:GE], dstE[:, 0:GE - 1], ALU.not_equal).then_inc(ne_made, 1)
            dve.wait_ge(last_made, 1)
            v.tensor_tensor(glast[:, :], wlast[:, :], iota_col[0:GROUPS, :], ALU.add).then_inc(last_made, 1)
            v.memset(recE[:, 0:1, 3:4], 1).then_inc(prep, 1)
            v.memset(brkE[:, 0, 0:1], -BIG).then_inc(prep, 1)
            v.memset(brkE[:, 1, GE - 1:GE], -BIG).then_inc(prep, 1)
            dve.wait_ge(last_made, 2)
            v.tensor_scalar(cmp[:, :], iota_row[0:GROUPS, 0:STEPS], glast[:, 0:1], None, ALU.is_gt).then_inc(cmp_made, 1)
            v.scalar_tensor_tensor(out=recE[:, :, 0], in0=srcE[:, :], scalar=float(R), in1=typE[:, :], op0=ALU.mult, op1=ALU.add).then_inc(cols_made, 1)
            v.tensor_copy(recE[:, :, 1], dstE[:, :]).then_inc(cols_made, 1)
            v.tensor_copy(recE[:, :, 2], typE[:, :]).then_inc(cols_made, 1)
            dve.wait_ge(cols_made, 3)
            v.tensor_copy(dst16[:, :], dstE[:, :]).then_inc(prep, 1)
            dve.wait_ge(ne_made, 1)
            v.tensor_copy(recE[:, 1:GE, 3], neE[:, 1:GE]).then_inc(prep, 1)
            v.tensor_scalar(brkE[:, 0, 1:GE], neE[:, 1:GE], -BIG, None, ALU.mult).then_inc(prep, 1)
            v.tensor_scalar(brkE[:, 1, 0:GE - 1], neE[:, 1:GE], -BIG, None, ALU.mult).then_inc(prep, 1)
            dve.wait_ge(attn_in, 32)
            for a in range(2):
                v.tensor_tensor(Bd[:, :, a * H:(a + 1) * H], headsel[:, :, :],
                                attn_col[:, a, :].unsqueeze(2).to_broadcast([P, 2, H]), ALU.mult).then_inc(bd_made, 1)
            dve.wait_ge(cnt_mm, 2)
            v.tensor_scalar(gcol[:, :], psE[0][0:STEPS, P:P + 1], float(GROUPS - 1), None, ALU.min).then_inc(gcol_made, 1)
            v.tensor_scalar(cnt[:, :], psE[0][:, 0:STEPS], float(GROUPS - 1), None, ALU.min).then_inc(tabs, 1)
            dve.wait_ge(tabs, 1)
            v.tensor_tensor(win[:, :], iota_row[:, 0:STEPS], cnt[:, :], ALU.subtract).then_inc(win_made, 1)
            dve.wait_ge(win_made, 2)
            v.tensor_copy(wtab[:, :], win[0:1, :]).then_inc(tabs, 1)
            v.tensor_scalar(node[:, :], win[:, :], float(P), pcol[:, 0:1], ALU.mult, ALU.add).then_inc(tabs, 1)
            v.tensor_scalar(win128[:, :], win[:, :], float(P), None, ALU.mult).then_inc(tabs, 1)
            v.tensor_tensor(keep[:, 1:STEPS], win[:, 1:STEPS], win[:, 0:STEPS - 1], ALU.is_equal).then_inc(keep_made, 1)

            def low_W(c):
                dve.wait_ge(wt_hi, c + 1)
                v.tensor_tensor(WT[1][:, :, c * P:(c + 1) * P], psH[c % 4][:, 0:256].rearrange("p (k n) -> p k n", k=KT),
                                WT[0][:, :, c * P:(c + 1) * P].bitcast(F32), ALU.subtract).then_inc(wt_lo, 1)

            dve.wait_ge(a_hi, 4)
            pa = psE[1][:, 0:256].rearrange("p (k r c) -> p k r c", k=KT, r=R)
            for k in range(KT):
                for lo, form, a in ((0, "p (r h) -> p r h", 0), (64, "p (h r) -> p r h", 1)):
                    v.tensor_tensor(A[1][:, k, lo:lo + 64].rearrange(form, r=R), pa[:, k, :, a * H:(a + 1) * H],
                                    A[0][:, k, lo:lo + 64].bitcast(F32).rearrange(form, r=R), ALU.subtract).then_inc(a_lo, 1)

            def low_xT(n, b, cb, j):
                dve.wait_ge(xt_hi, n + 1)
                v.tensor_tensor(xTs[:, cb, j, 1, :], psX[b][:, 0:256], xTs[:, cb, j, 0, :].bitcast(F32), ALU.subtract).then_inc(xt_lo, 1)

            def low_scores(n, b, cb, j):
                dve.wait_ge(ssrc_out, n + 1)
                if not (isinstance(n, int) and n < 2):
                    dve.wait_ge(sd_parts, (n - 1) * 2)
                v.tensor_tensor(sdr[:, b, :], psE[b][:, 320:384], sdo[:, cb, j, 0, :], ALU.subtract).then_inc(sd_lo, 1)
                dve.wait_ge(sd_lo, n + 1)
                v.tensor_copy(sdo[:, cb, j, 1, :], sdr[:, b, :]).then_inc(sd_parts, 1)
                dve.wait_ge(sd_parts, n * 2 + 1)
                v.tensor_tensor(sdo[:, cb, j, 2, :], sdr[:, b, :], sdo[:, cb, j, 1, :], ALU.subtract).then_inc(sd_parts, 1)

            def low_chunk(c, cb, stored, tiles=C):
                if stored is not None:
                    dve.wait_ge(chunk_st[cb], stored)
                for j in range(tiles):
                    low_xT(c * C + j, j % 2, cb, j)
                    if isinstance(c, int) and c < 2:
                        low_W((c * C + j) * 2)
                        low_W((c * C + j) * 2 + 1)
                    if j:
                        low_scores(c * C + j - 1, (j - 1) % 2, cb, j - 1)
                low_scores(c * C + tiles - 1, (tiles - 1) % 2, cb, tiles - 1)

            low_chunk(0, 0, None)
            low_chunk(1, 1, None)
            with dve.Fori(1, CHUNKS // 2) as i:
                for cb in range(2):
                    low_chunk(i * 2 + cb, cb, i * 32)
            low_chunk(CHUNKS, 0, 32 * (CHUNKS // 2), 1)

            def oht_step(s, j, b, n, cond):
                dve.wait_ge(drow_in[j], n)
                if cond is not None:
                    dve.wait_ge(sd_mm, cond)
                v.tensor_scalar(ohT[:, b, :], drow[:, j, :], node[:, ds(s, 1)], None, ALU.is_equal).then_inc(oht, 1)
                v.tensor_tensor(rmask[:, b, :, :], rec[:, ds(s, 1), :, 2:3].rearrange("p a t c -> p (a t) c").to_broadcast([EP, T, R]),
                                iota_row[0:EP, 0:R].unsqueeze(1).to_broadcast([EP, T, R]), ALU.is_equal).then_inc(rm_made, 1)

            def pick_step(s, b):
                dve.wait_ge(sd_mm, s + 1)
                dve.wait_ge(rm_made, s + 1)
                v.tensor_tensor(sdm[:, b, :, :].rearrange("p (t h) r -> p t h r", t=T),
                                psE[b][0:EP, 0:256].rearrange("p (t h r) -> p t h r", t=T, h=H),
                                rmask[:, b, :, :].unsqueeze(2).to_broadcast([EP, T, H, R]), ALU.mult).then_inc(sdm_made, 1)
                dve.wait_ge(sdm_made, s + 1)
                v.tensor_reduce(sdS[:, ds(s, 1), :, :].rearrange("p a t h -> p (a t h)"), sdm[:, b, :, :],
                                axis=AXX, op=ALU.add).then_inc(sd_done, 1)

            dve.wait_ge(rec_in, 16 * Q)
            oht_step(0, 0, 0, 16, None)
            oht_step(1, 1, 1, 16, None)
            pick_step(0, 0)
            with dve.Fori(0, SWEEPS) as i:
                for j in range(2 * PRE):
                    s = i * (2 * PRE) + j + 2
                    oht_step(s, (j + 2) % PRE, j % 2, (i * 2 + (j + 2) // PRE + 1) * 16, s - 1)
                    pick_step(s - 1, (j + 1) % 2)
            for s in (STEPS - 2, STEPS - 1):
                oht_step(s, s % PRE, s % 2, (s // PRE + 1) * 16, s - 1)
                pick_step(s - 1, (s - 1) % 2)
            pick_step(STEPS - 1, 1)
            dve.wait_ge(sd_done, STEPS)
            dve.wait_ge(keep_made, 3)

            for b, n in ((0, SWEEPS + 1), (1, SWEEPS)):
                dve.wait_ge(h_st[b], 16 * n)
            v.memset(brk[:, :, :, :], 0.0).then_inc(zeroed, 1)
            v.memset(accS[:, :, :], 0.0).then_inc(acc_made, 2)
            v.memset(s4[:, :, :, :], 0.0).then_inc(zeroed, 1)
            v.memset(M[:, :, :], 0.0).then_inc(mnew, 1)
            v.memset(dab[:, :, :], 0.0).then_inc(dab_made, 2)
            dve.wait_ge(mnew, 1)
            dve.wait_ge(dab_made, 2)
            dve.wait_ge(acc_made, 2)
            v.memset(xres[:, WINDOWS - 1, :], 0.0).then_inc(zeroed, 1)
            dve.wait_ge(zeroed, 3)

            def scores(q, z, n):
                for g in range(Q):
                    dve.wait_ge(gath[z][g], n)
                gs = G[:, z, :, 0:ROW].rearrange("p (g t) (h d) -> p g t h d", g=Q, h=H)
                for g in range(Q):
                    i_ = v.tensor_tensor(sraw[:, :, :].rearrange("p (t g) h -> p g t h", g=Q)[:, g, :, :], gs[:, g, :, :, D],
                                         sdS[:, ds(q * Q + g, 1), :, :].rearrange("p a t h -> p (a t) h"), ALU.add)
                i_.then_inc(sraw_made, 1)
                dve.wait_ge(sraw_made, q + 1)
                v.scalar_tensor_tensor(out=s4[:, :, :, 0:H].rearrange("p t g h -> p (t g) h"), in0=sraw[:, :, :],
                                       scalar=NEG_SLOPE, in1=sraw[:, :, :], op0=ALU.mult, op1=ALU.max).then_inc(s4_made, 1)

            def scans(q, b, n):
                dve.wait_ge(sT_out, q + 1)
                dve.wait_ge(brk_in[b], n)
                v.tensor_tensor_scan(fwd[:, :], brk[:, b, 0, :], sT[:, :], -BIG, ALU.add, ALU.max).then_inc(fwd_made, 1)
                dve.wait_ge(fwd_made, q + 1)
                if not (isinstance(q, int) and q == 0):
                    dve.wait_ge(m_mm, q)
                v.tensor_tensor_scan(mT[:, ::-1], brk[:, b, 1, ::-1], fwd[:, ::-1], -BIG, ALU.add, ALU.max).then_inc(mT_made, 1)

            def shifted(q, z):
                dve.wait_ge(m_mm, q + 1)
                pm = psM[0:EP, :].rearrange("p (c h) -> p c h", h=PAD)[:, :, 0:H]
                if not (isinstance(q, int) and q == 0):
                    dve.wait_ge(w_made, q)
                v.tensor_tensor(dif[:, :, :], s4[:, :, :, 0:H].rearrange("p t g h -> p (t g) h"), pm, ALU.subtract).then_inc(dif_made, 1)
                v.tensor_tensor(G[:, z, :, ROW:GROW].rearrange("p (g t) h -> p g t h", g=Q),
                                pm.rearrange("p (t g) h -> p g t h", g=Q),
                                rec[:, ds(q * Q, Q), :, 3:4].to_broadcast([EP, Q, T, H]), ALU.mult).then_inc(first_made, 1)

            def messages(q, z, g):
                s = q * Q + g
                v.scalar_tensor_tensor(out=onehot[:, g % 2, :, :],
                                       in0=rec[:, ds(s, 1), :, 1:2].rearrange("p a t c -> p (a t) c").to_broadcast([EP, T, P]),
                                       scalar=win128[0:EP, ds(s, 1)],
                                       in1=iota_row[0:EP, :].unsqueeze(1).to_broadcast([EP, T, P]),
                                       op0=ALU.subtract, op1=ALU.is_equal).then_inc(oh_made, 1)
                dve.wait_ge(w_made, q + 1)
                f = G[:, z, g * T:(g + 1) * T, 0:ROW].rearrange("p t (h d) -> p t h d", h=H)
                v.tensor_tensor(f[:, :, :, 0:D], f[:, :, :, 0:D], f[:, :, :, D:HD].to_broadcast([EP, T, H, D]), ALU.mult).then_inc(msg_made, 1)

            def maxima(q, g):
                s = q * Q + g
                b, o_ = g % 2, (g + 1) % 2
                dve.wait_ge(p_mm, s + 1)
                dve.wait_ge(mnew, s + 1)
                dve.wait_ge(dab_made, s * 2 + 2)
                k = keep[:, ds(s, 1)]
                ms = psP[g][:, ROW:GROW]
                v.scalar_tensor_tensor(out=M[:, b, :], in0=M[:, o_, :], scalar=k, in1=ms, op0=ALU.mult, op1=ALU.max).then_inc(mnew, 1)
                dve.wait_ge(mnew, s + 2)
                v.scalar_tensor_tensor(out=dab[:, b, 0:H], in0=M[:, o_, :], scalar=k, in1=M[:, b, :], op0=ALU.mult, op1=ALU.subtract).then_inc(dab_made, 1)
                v.tensor_tensor(dab[:, b, H:2 * H], ms, M[:, b, :], ALU.subtract).then_inc(dab_made, 1)

            def merge(q, g):
                s = q * Q + g
                b = g % 2
                dve.wait_ge(scaled, s + 1)
                dve.wait_ge(acc_made, s + 2)
                dve.wait_ge(acc_st, s * 16 + 16)
                v.scalar_tensor_tensor(out=accS[:, b, :].rearrange("p (h d) -> p h d", h=H),
                                       in0=accS[:, (g + 1) % 2, :].rearrange("p (h d) -> p h d", h=H), scalar=keep[:, ds(s, 1)],
                                       in1=eab[:, b, 0:H].unsqueeze(2).to_broadcast([P, H, HD]), op0=ALU.mult, op1=ALU.mult).then_inc(acc_scaled, 1)
                dve.wait_ge(acc_scaled, s + 1)
                v.tensor_tensor(accS[:, b, :], accS[:, b, :], tsum[:, b, :], ALU.add).then_inc(acc_made, 1)

            scores(0, 0, 16 * T)
            scans(0, 0, 16 * Q)
            shifted(0, 0)
            def quad(q, c, gathered, broken, before=True):
                zq, zp = (c + 1) % SLOTS, c % SLOTS
                messages(q - 1, zp, 0)
                if before:
                    maxima(q - 2, 3)
                    merge(q - 2, 2)
                scores(q, zq, gathered)
                messages(q - 1, zp, 1)
                maxima(q - 1, 0)
                if before:
                    merge(q - 2, 3)
                scans(q, (c + 1) % 2, broken)
                messages(q - 1, zp, 2)
                maxima(q - 1, 1)
                merge(q - 1, 0)
                shifted(q, zq)
                messages(q - 1, zp, 3)
                maxima(q - 1, 2)
                merge(q - 1, 1)

            for q in range(1, 2 * SLOTS + 1):
                quad(q, q - 1, (q // SLOTS + 1) * 16 * T, (q // 2 + 1) * 16 * Q, q > 1)
            with dve.Fori(1, (QUADS - 1) // (2 * SLOTS)) as i:
                for c in range(2 * SLOTS):
                    quad(i * (2 * SLOTS) + c + 1, c, (i * 2 + (c + 1) // SLOTS + 1) * 16 * T, (i * SLOTS + (c + 1) // 2 + 1) * 16 * Q)
            zl = (QUADS - 1) % SLOTS
            messages(QUADS - 1, zl, 0)
            maxima(QUADS - 2, 3)
            merge(QUADS - 2, 2)
            for g in range(1, Q):
                messages(QUADS - 1, zl, g)
                maxima(QUADS - 1, g - 1)
                if g == 1:
                    merge(QUADS - 2, 3)
                else:
                    merge(QUADS - 1, g - 2)
            maxima(QUADS - 1, Q - 1)
            merge(QUADS - 1, Q - 2)
            merge(QUADS - 1, Q - 1)

            dve.wait_ge(acc_st, 16 * (STEPS + 2))

            def divide(c):
                cs = slice(c * PRE, (c + 1) * PRE)
                if c:
                    dve.wait_ge(y_made, c)
                v.tensor_scalar(rden[:, :, :], accW[:, cs, :, D], DENOM_EPS, None, ALU.add).then_inc(rd_made, 1)
                dve.wait_ge(rd_made, 2 * c + 1)
                v.reciprocal(rden[:, :, :], rden[:, :, :]).then_inc(rd_made, 1)
                dve.wait_ge(rd_made, 2 * c + 2)
                a = accW[:, cs, :, 0:D].rearrange("p w h d -> p (w h) d")
                v.tensor_tensor(a, a, rden[:, :, :].rearrange("p w h -> p (w h)").unsqueeze(2).to_broadcast([P, PRE * H, D]), ALU.mult).then_inc(y_made, 1)

            def statistics(c):
                dve.wait_ge(ysum_made, c + 1)
                if c:
                    dve.wait_ge(o_made, PRE * c)
                for j in range(PRE):
                    v.bn_stats(st[:, j, :], xres[:, c * PRE + j, :]).then_inc(stats_made, 1)
                dve.wait_ge(stats_made, PRE * (c + 1))
                for j in range(PRE):
                    v.bn_aggr(mv[:, j, :], st[:, j, :]).then_inc(mv_made, 1)
                dve.wait_ge(root_made, c + 1)
                v.reciprocal(rstd[:, :], rstd[:, :]).then_inc(rstd_made, 1)
                dve.wait_ge(rstd_made, 2 * c + 1)
                v.scalar_tensor_tensor(out=mv[:, :, 0], in0=mv[:, :, 0], scalar=-1.0, in1=rstd[:, :], op0=ALU.mult, op1=ALU.mult).then_inc(rstd_made, 1)

            divide(0)
            for c in range(WINDOWS // PRE):
                if c + 1 < WINDOWS // PRE:
                    divide(c + 1)
                statistics(c)


def kernel(x, src, dst, edge_type_8, L0_gnn_W, L0_gnn_attn_src, L0_gnn_attn_dst):
    import concourse.bacc as bacc
    from concourse import mybir
    from concourse.bass_utils import run_bass_kernel_spmd

    nc = bacc.Bacc("TRN2", target_bir_lowering=False, num_devices=1)
    named = {"x": x, "src": src, "dst": dst, "etype": edge_type_8, "W": L0_gnn_W,
             "attn_src": L0_gnn_attn_src, "attn_dst": L0_gnn_attn_dst}
    arrays, aps = {}, {}
    for name, a in named.items():
        a = np.ascontiguousarray(a)
        arrays[f"in_{name}"] = a
        aps[name] = nc.dram_tensor(f"in_{name}", a.shape, mybir.dt.from_np(a.dtype), kind="ExternalInput").ap()
    out = nc.dram_tensor("out_0", (N, F), mybir.dt.float32, kind="ExternalOutput").ap()
    gnn_kernel(nc, out=out, **aps)
    r = run_bass_kernel_spmd(nc, [arrays], core_ids=[0])
    return r.results[0]["out_0"]
```

```python
import numpy as np

N, F = 3125, 256
R, H, D = 8, 8, 32
E = 50000
NEG_SLOPE = 0.2
DENOM_EPS = 1e-12
LN_EPS = 1e-5

P = 128
KT = F // P
WINDOWS = -(-N // P)
TAIL = N - (WINDOWS - 1) * P
EP = 125
T = 4
GE = EP * T
GROUPS = E // GE
STEPS = GROUPS - 1 + WINDOWS
Q = 4
QUADS = STEPS // Q
SLOTS = 3
ROW = F + H
HD = D + 1
GROW = ROW + H
C = 4
PRE = 5
PAD = 32
BIG = 1e30
SPRAY = EP // 16 * 16
TAIL_SPRAY = TAIL // 16 * 16
PARTS = [(0, 5), (5, 5), (10, 5), (15, 5), (20, 4), (24, 1)]
EARLY = 4
MAGIC = 0x5F3759DF
NEWTON = 3
assert GROUPS * GE == E and QUADS * Q == STEPS and PRE * WINDOWS == STEPS + 1
assert (QUADS - 1) % SLOTS == 0 and WINDOWS % (2 * C) == 1


def gnn_kernel(nc, x, src, dst, etype, W, attn_src, attn_dst, out):
    import concourse.bass as bass
    from concourse import mybir
    from contextlib import ExitStack

    ALU = mybir.AluOpType
    ACT = mybir.ActivationFunctionType
    F32 = mybir.dt.float32
    F32R = mybir.dt.float32r
    BF16 = mybir.dt.bfloat16
    I32 = mybir.dt.int32
    I16 = mybir.dt.int16
    AXX = mybir.AxisListType.X
    ds = bass.ds

    with ExitStack() as ctx:
        def sb(name, shape, dt=F32, c=ctx):
            return c.enter_context(nc.sbuf_tensor(name, shape, dt))

        def ps(name):
            return ctx.enter_context(nc.psum_tensor(name, [P, 512], F32))

        def sem(name):
            return ctx.enter_context(nc.semaphore(name))

        def dram(name, shape, dt=F32):
            return nc.dram_tensor(name, shape, dt, kind="Internal").ap()

        table = dram("table", [N * R, ROW])
        rec_d = dram("rec_d", [GROUPS, EP, T * 4], I32)
        brk_d = dram("brk_d", [GROUPS, 2 * GE])
        recs_d = dram("recs_d", [STEPS, EP, T * 4], I32)
        brks_d = dram("brks_d", [STEPS, 2 * GE])
        dstrows_d = dram("dstrows_d", [STEPS, GE], I16)
        dstrow_d = dram("dstrow_d", [GROUPS, GE], I16)
        sorted_d = dram("sorted_d", [E, 3], I32)
        xT_d = dram("xT_d", [WINDOWS, P, 2 * KT * P])
        sdst_d = dram("sdst_d", [WINDOWS, P, 3 * H * R], BF16)

        ident = sb("ident", [P, P])
        iota_row = sb("iota_row", [P, P], I32)
        iota_col = sb("iota_col", [P, 1], I32)
        pcol = sb("pcol", [P, 1])
        cnt = sb("cnt", [P, STEPS])
        win = sb("win", [P, STEPS])
        win128 = sb("win128", [P, STEPS])
        node = sb("node", [P, STEPS])
        keep = sb("keep", [P, STEPS])
        wtab = sb("wtab", [1, STEPS], I32)
        rec = sb("rec", [EP, STEPS, T, 4], I32)
        sdS = sb("sdS", [EP, STEPS, T, H])

        build = ExitStack()
        ones = sb("ones", [P, P], c=build)
        headsel = sb("headsel", [P, 2, H], c=build)
        attn_col = sb("attn_col", [P, 2, 2], c=build)
        Bd = sb("Bd", [P, 2, 2 * H], c=build)
        Wnat = sb("Wnat", [P, 2 * R, F], c=build)
        WT = [sb(f"WT{l}", [P, KT, R * F], F32R, build) for l in "hl"]
        A = [sb(f"A{l}", [P, KT, 2 * H * R], F32R, build) for l in "hl"]
        dstE = sb("dstE", [GROUPS, GE], I32, build)
        srcE = sb("srcE", [GROUPS, GE], I32, build)
        typE = sb("typE", [GROUPS, GE], I32, build)
        recE = sb("recE", [GROUPS, GE, 4], I32, build)
        neE = sb("neE", [GROUPS, GE], c=build)
        brkE = sb("brkE", [GROUPS, 2, GE], c=build)
        dst16 = sb("dst16", [GROUPS, GE], I16, build)
        nxt = sb("nxt", [GROUPS, 2], I32, build)
        bad = sb("bad", [GROUPS, 2], c=build)
        unsorted = sb("unsorted", [1, 1], I32, build)
        own = sb("own", [EP, GROUPS * T], I32, build)
        srt = sb("srt", [EP, GROUPS * T, 3], I32, build)
        thr = sb("thr", [EP, GROUPS * T], c=build)
        places = sb("places", [EP, GROUPS * T], I32, build)
        rowb = sb("rowb", [EP, GE], I32, build)
        before = sb("before", [EP, T, GE], BF16, build)
        less = sb("less", [EP, T, GE], BF16, build)
        less_n = sb("less_n", [EP, T], c=build)
        place = sb("place", [EP, 1], I32, build)
        record = sb("record", [EP, 3], I32, build)
        gcol = sb("gcol", [STEPS, 1], I32, build)
        recS = sb("recS", [STEPS, EP * T * 4], I32, build)
        brkS = sb("brkS", [STEPS, 2 * GE], c=build)
        dstS = sb("dstS", [STEPS, GE], I16, build)
        wlast = sb("wlast", [GROUPS, 1], I32, build)
        glast = sb("glast", [GROUPS, 1], c=build)
        cmp = sb("cmp", [GROUPS, STEPS], c=build)
        xin = sb("xin", [P, 2, C, F], c=build)
        xTs = sb("xTs", [P, 2, C, 2, KT * P], F32R, build)
        sdo = sb("sdo", [P, 2, C, 3, H * R], BF16, build)
        sdr = sb("sdr", [P, 2, H * R], c=build)
        ssrc = sb("ssrc", [P, WINDOWS, R * H], c=build)
        xT = sb("xT", [P, 2, 2, KT, P], F32R, build)
        hbuf = sb("hbuf", [P, 2, R, H, HD], c=build)
        drow = sb("drow", [P, PRE, GE], I16, build)
        sdw = sb("sdw", [P, PRE, 3, H * R], BF16, build)
        ohT = sb("ohT", [P, 2, GE], BF16, build)
        rmask = sb("rmask", [EP, 2, T, R], c=build)
        sdm = sb("sdm", [EP, 2, T * H, R], c=build)
        build.close()

        G = sb("G", [EP, SLOTS, Q * T, GROW])
        idx = sb("idx", [EP, SLOTS, Q * T], I32)
        sraw = sb("sraw", [EP, T * Q, H])
        s4 = sb("s4", [EP, T, Q, PAD])
        sT = sb("sT", [P, GE])
        fwd = sb("fwd", [P, GE])
        mT = sb("mT", [P, GE])
        brk = sb("brk", [P, 2, 2, GE])
        dif = sb("dif", [EP, T * Q, H])
        onehot = sb("onehot", [EP, 2, T, P])
        M = sb("M", [P, 2, H])
        dab = sb("dab", [P, 2, 2 * H])
        eab = sb("eab", [P, 2, 2 * H])
        accS = sb("accS", [P, 2, ROW])
        tsum = sb("tsum", [P, 2, ROW])
        accW = sb("accW", [P, WINDOWS, H, HD])
        xres = sb("xres", [P, WINDOWS, F])
        rden = sb("rden", [P, WINDOWS, H])
        st = sb("st", [P, WINDOWS, 6])
        mv = sb("mv", [P, WINDOWS, 2])
        vare = sb("vare", [P, WINDOWS])
        half = sb("half", [P, WINDOWS], I32)
        newt = sb("newt", [P, WINDOWS])
        rstd = sb("rstd", [P, WINDOWS])
        shift = sb("shift", [P, WINDOWS])

        psX = [ps(f"psX{b}") for b in range(2)]
        psH = [ps(f"psH{b}") for b in range(4)]
        psE = [ps(f"psE{b}") for b in range(2)]
        psT, psM = psX
        psP = psH

        flag_steps, bad_mm, edges_ok = sem("flag_steps"), sem("bad_mm"), sem("edges_ok")
        sort_in, row_in, row_used, before_made = sem("sort_in"), sem("row_in"), sem("row_used"), sem("before_made")
        srt_made, thr_made, less_made, less_sum, place_made = sem("srt_made"), sem("thr_made"), sem("less_made"), sem("less_sum"), sem("place_made")
        column_used, record_made, sort_out, back = sem("column_used"), sem("record_made"), sem("sort_out"), sem("back")
        edges_in, w_in, attn_in = sem("edges_in"), sem("w_in"), sem("attn_in")
        consts0, consts = sem("consts0"), sem("consts")
        prep, rec_out, tabs = sem("prep"), sem("rec_out"), sem("tabs")
        ne_made, last_made, cols_made = sem("ne_made"), sem("last_made"), sem("cols_made")
        cmp_made, win_made, keep_made, cnt_mm = sem("cmp_made"), sem("win_made"), sem("keep_made"), sem("cnt_mm")
        bd_made, a_mm, a_hi, a_lo = sem("bd_made"), sem("a_mm"), sem("a_hi"), sem("a_lo")
        wt_mm, wt_hi, wt_lo = sem("wt_mm"), sem("wt_hi"), sem("wt_lo")
        x_in = [sem(f"x_in{b}") for b in range(2)]
        xt_mm, xt_hi, xt_lo = sem("xt_mm"), sem("xt_hi"), sem("xt_lo")
        sc_mm, ssrc_out, sd_hi, sd_lo = sem("sc_mm"), sem("ssrc_out"), sem("sd_hi"), sem("sd_lo")
        chunk_st = [sem(f"chunk_st{b}") for b in range(2)]
        xT_in = [sem(f"xT_in{b}") for b in range(2)]
        h_mm, h_out, hs_out = sem("h_mm"), sem("h_out"), sem("hs_out")
        h_st = [sem(f"h_st{b}") for b in range(2)]
        drow_in = [sem(f"drow_in{b}") for b in range(PRE)]
        sdw_in = [sem(f"sdw_in{b}") for b in range(PRE)]
        sd_parts = sem("sd_parts")
        rec_in, gcol_made, steps_in = sem("rec_in"), sem("gcol_made"), sem("steps_in")
        dsts_out, recs_out, brks_out = sem("dsts_out"), sem("recs_out"), sem("brks_out")
        oht, rm_made, sd_mm, sdm_made, sd_done = sem("oht"), sem("rm_made"), sem("sd_mm"), sem("sdm_made"), sem("sd_done")
        idx_made = sem("idx_made")
        gath = [[sem(f"gath{z}_{g}") for g in range(Q)] for z in range(SLOTS)]
        zeroed, xres_in = sem("zeroed"), sem("xres_in")
        sraw_made, s4_made = sem("sraw_made"), sem("s4_made")
        sT_mm, sT_out = sem("sT_mm"), sem("sT_out")
        brk_in = [sem(f"brk_in{b}") for b in range(2)]
        fwd_made, mT_made, m_mm = sem("fwd_made"), sem("mT_made"), sem("m_mm")
        dif_made, w_made, first_made = sem("dif_made"), sem("w_made"), sem("first_made")
        oh_made, msg_made, p_mm = sem("oh_made"), sem("msg_made"), sem("p_mm")
        mnew, dab_made, eab_made = sem("mnew"), sem("dab_made"), sem("eab_made")
        acc_scaled = sem("acc_scaled")
        scaled, acc_made, acc_st = sem("scaled"), sem("acc_made"), sem("acc_st")
        rd_made, y_made, ysum_made, stats_made = sem("rd_made"), sem("y_made"), sem("ysum_made"), sem("stats_made")
        mv_made, root_steps, shift_made, o_st = sem("mv_made"), sem("root_steps"), sem("shift_made"), sem("o_st")
        o_act, o_pool, o_dve = sem("o_act"), sem("o_pool"), sem("o_dve")

        block = ctx.enter_context(nc.Block())

        TABS = 4
        SWEEPS = (WINDOWS - 1) // 2
        CHUNKS = (WINDOWS - 1) // C

        @block.sync
        def _(sp):
            sp.dma_start(dstE[:, :], dst.rearrange("(g e) -> g e", g=GROUPS)).then_inc(edges_in, 16)
            sp.wait_ge(flag_steps, 1)
            sp.dma_start(nxt[0:GROUPS - 1, :], dst.rearrange("(g e) -> g e", g=GROUPS)[1:GROUPS, 0:2]).then_inc(edges_in, 16)
            for r in range(R):
                sp.dma_start(Wnat[:, 2 * r:2 * r + 2, :], W[r].rearrange("(a o) f -> o a f", a=2)).then_inc(w_in, 16)
            sp.dma_start(srcE[:, :], src.rearrange("(g e) -> g e", g=GROUPS)).then_inc(edges_in, 16)
            sp.dma_start(typE[:, :], etype.rearrange("(g e) -> g e", g=GROUPS)).then_inc(edges_in, 16)
            sp.wait_ge(prep, 7)
            sp.dma_start(rec_d.rearrange("g p c -> g (p c)"), recE[:, :, :].rearrange("g e c -> g (e c)")).then_inc(rec_out, 16)
            sp.dma_start(brk_d, brkE[:, :, :].rearrange("g a e -> g (a e)")).then_inc(rec_out, 16)
            sp.dma_start(dstrow_d, dst16[:, :]).then_inc(rec_out, 16)
            sp.wait_ge(rec_out, 48)
            sp.wait_ge(steps_in, 48)
            sp.dma_start(dstrows_d, dstS[:, :]).then_inc(dsts_out, 16)
            sp.dma_start(recs_d.rearrange("s p c -> s (p c)"), recS[:, :]).then_inc(recs_out, 16)
            sp.dma_start(brks_d, brkS[:, :]).then_inc(brks_out, 16)
            sp.wait_ge(recs_out, 16)
            sp.wait_ge(xt_mm, 4 * C)
            for k in range(Q):
                ks = slice(k * QUADS, (k + 1) * QUADS)
                for ps_ in (slice(0, SPRAY), slice(SPRAY, EP)):
                    sp.dma_start(rec[ps_, ks, :, :].rearrange("p s t c -> p s (t c)"),
                                 recs_d[ks, ps_].rearrange("s p c -> p s c")).then_inc(rec_in, 16)

            sp.wait_ge(tabs, TABS)
            for b in range(2):
                sp.wait_ge(chunk_st[b], 32)

            def stage_scores(s, j, cond):
                w = sp.value_load(wtab[0:1, ds(s, 1)], min_val=0, max_val=WINDOWS - 1)
                if cond is not None:
                    sp.wait_ge(sd_mm, cond)
                sp.dma_start(sdw[:, j, :, :].rearrange("p a c -> p (a c)"),
                             sdst_d[ds(w, 1), :, :].rearrange("a p c -> p (a c)")).then_inc(sdw_in[j], 16)

            for j in range(PRE):
                stage_scores(j, j, None)
            for b, n in ((0, CHUNKS // 2 + 1), (1, CHUNKS // 2)):
                sp.wait_ge(chunk_st[b], 32 * n)
            with sp.Fori(1, WINDOWS - 1) as i:
                for j in range(PRE):
                    stage_scores(i * PRE + j, j, i * PRE + j + 1 - PRE)
            for j in range(PRE - 1):
                s = (WINDOWS - 1) * PRE + j
                stage_scores(s, j, s + 1 - PRE)
            sp.wait_ge(brks_out, 16)

            def breaks(q, b):
                for g_ in range(Q):
                    sp.dma_start(brk[g_ * PAD:g_ * PAD + H, b, :, :].rearrange("p a e -> p (a e)"),
                                 brks_d[ds(q * Q + g_, 1), :].to_broadcast([H, 2 * GE])).then_inc(brk_in[b], 16)

            def keep_acc(s, b):
                w = sp.value_load(wtab[0:1, ds(s, 1)], min_val=0, max_val=WINDOWS - 1)
                sp.wait_ge(acc_made, s + 3)
                sp.wait_ge(acc_st, s * 16 + 32)
                sp.dma_start(accW[:, ds(w, 1), :, :].rearrange("p a h d -> p (a h d)"), accS[:, b, :]).then_inc(acc_st, 16)

            sp.wait_ge(zeroed, 3)
            sp.wait_ge(acc_made, 2)
            breaks(0, 0)
            breaks(1, 1)
            for b in range(2):
                sp.dma_start(accW[:, b, :, :].rearrange("p h d -> p (h d)"), accS[:, b, :]).then_inc(acc_st, 16)
                sp.wait_ge(acc_st, 16 * (b + 1))
            sp.dma_start(xres[:, 0:WINDOWS - 1, :], x[0:(WINDOWS - 1) * P, :].rearrange("(w p) f -> p w f", p=P)).then_inc(xres_in, 16)
            sp.dma_start(xres[0:TAIL, WINDOWS - 1, :], x[(WINDOWS - 1) * P:N, :]).then_inc(xres_in, 16)
            def quad(q, b):
                for g_ in range(Q):
                    if g_ == 2:
                        sp.wait_ge(mT_made, q - 1)
                        breaks(q, b)
                    keep_acc((q - 2) * Q + g_, g_ % 2)

            quad(2, 0)
            with sp.Fori(1, (QUADS - 1) // 2) as i:
                for b in range(2):
                    quad(i * 2 + b + 1, (b + 1) % 2)
            for s in range((QUADS - 2) * Q, STEPS - 1):
                keep_acc(s, s % 2)

            for c, (w0, n) in enumerate(PARTS):
                sp.wait_ge((o_act, o_pool, o_dve)[c // 2], w0 + n - PARTS[c // 2 * 2][0])
                if w0 + n < WINDOWS:
                    sp.dma_start(out[w0 * P:(w0 + n) * P, :].rearrange("(w p) f -> p w f", p=P), xres[:, w0:w0 + n, :]).then_inc(o_st, 16)
                else:
                    for lo, hi in ((0, TAIL_SPRAY), (TAIL_SPRAY, TAIL)):
                        sp.dma_start(out[w0 * P + lo:w0 * P + hi, :], xres[lo:hi, w0, :]).then_inc(o_st, 16)
            sp.wait_ge(o_st, 16 * (len(PARTS) + 1))

        @block.gpsimd
        def _(pool):
            nc.gpsimd.memset(ident[:, :], 0.0).then_inc(consts0, 1)
            nc.gpsimd.memset(headsel[:, :, :], 1.0).then_inc(consts0, 1)
            nc.gpsimd.iota(iota_row[:, :], pattern=[[1, P]], base=0, channel_multiplier=0).then_inc(consts, 1)
            nc.gpsimd.iota(iota_col[:, :], pattern=[[1, 1]], base=0, channel_multiplier=1).then_inc(consts, 1)
            nc.gpsimd.memset(ones[:, :], 1.0).then_inc(consts, 1)
            pool.wait_ge(consts0, 2)
            nc.gpsimd.affine_select(out=ident[:, :], in_=ident[:, :], compare_op=ALU.not_equal, fill=1.0,
                                    base=0, pattern=[[-1, P]], channel_multiplier=1).then_inc(consts, 1)
            nc.gpsimd.affine_select(out=headsel[:, :, :], in_=headsel[:, :, :], compare_op=ALU.is_ge, fill=0.0,
                                    base=0, pattern=[[P, 2], [-D, H]], channel_multiplier=1).then_inc(consts0, 1)
            pool.wait_ge(consts0, 3)
            nc.gpsimd.affine_select(out=headsel[:, :, :], in_=headsel[:, :, :], compare_op=ALU.is_ge, fill=0.0,
                                    base=D - 1, pattern=[[-P, 2], [D, H]], channel_multiplier=-1).then_inc(consts, 1)

            pool.wait_ge(flag_steps, 5)
            pool.wait_ge(edges_in, 64)
            flag = pool.value_load(unsorted[0:1, 0:1], min_val=0, max_val=GROUPS)
            with pool.If(flag):
                edge_columns = lambda a: a.rearrange("(g p t) -> p g t", p=EP, t=T)

                def bring(a):
                    for gs_ in (slice(b * GROUPS // 4, (b + 1) * GROUPS // 4) for b in range(4)):
                        pool.dma_start(own[:, :].rearrange("p (g t) -> p g t", t=T)[:, gs_, :], edge_columns(a)[:, gs_, :]).then_inc(sort_in, 16)

                bring(dst)
                nc.gpsimd.memset(before[:, :, :], 1.0).then_inc(before_made, 1)
                pool.wait_ge(before_made, 1)
                nc.gpsimd.affine_select(out=before[:, :, :], in_=before[:, :, :], compare_op=ALU.is_gt, fill=0.0,
                                        base=0, pattern=[[1, T], [-1, GE]], channel_multiplier=T).then_inc(before_made, 1)
                with pool.Fori(0, GROUPS) as i:
                    pool.wait_ge(row_used, i + 1)
                    pool.dma_start(rowb[:, :], dst.rearrange("(g e) -> g e", g=GROUPS)[ds(i, 1), :].to_broadcast([EP, GE])).then_inc(row_in, 16)
                for n, a in ((1, src), (2, etype)):
                    pool.wait_ge(column_used, n)
                    bring(a)
                pool.wait_ge(column_used, 4)
                with pool.Fori(0, GROUPS * T) as i:
                    nc.gpsimd.tensor_copy(place[:, :], places[:, ds(i, 1)]).then_inc(record_made, 1)
                    nc.gpsimd.tensor_copy(record[:, :], srt[:, ds(i, 1), :].rearrange("p a c -> p (a c)")).then_inc(record_made, 1)
                    pool.wait_ge(record_made, i * 2 + 2)
                    pool.nop(nofuse=True)
                    nc.gpsimd.indirect_dma_start(sorted_d, bass.IndirectOffsetOnAxis(ap=place[:, 0:1], axis=0), record[:, :], None).then_inc(sort_out, 16)
                    pool.wait_ge(sort_out, i * 16 + 16)
                    pool.nop(nofuse=True)
                back_rows = recS[0:GROUPS, 0:3 * GE]
                pool.dma_start(back_rows, sorted_d.rearrange("(g e) c -> g (e c)", g=GROUPS)).then_inc(sort_in, 16)
                pool.wait_ge(sort_in, 16 * 13)
                for m, a in enumerate((srcE, dstE, typE)):
                    nc.gpsimd.tensor_copy(a[:, :], back_rows.rearrange("g (e c) -> g e c", c=3)[:, :, m]).then_inc(back, 1)
                pool.wait_ge(back, 3)
            pool.nop(nofuse=True).then_inc(edges_ok, 1)

            pool.wait_ge(rec_out, 48)
            pool.wait_ge(gcol_made, 1)
            pool.nop(nofuse=True)
            for rows, table_d in ((dstS, dstrow_d), (recS, rec_d.rearrange("g p c -> g (p c)")), (brkS, brk_d)):
                nc.gpsimd.indirect_dma_start(rows[:, :], None, table_d,
                                             bass.IndirectOffsetOnAxis(ap=gcol[:, 0:1], axis=0)).then_inc(steps_in, 16)

            def stage(s, j, cond):
                if cond is not None:
                    pool.wait_ge(oht, cond)
                pool.dma_start(drow[:, j, :], dstrows_d[ds(s, 1), :].to_broadcast([P, GE])).then_inc(drow_in[j], 16)

            pool.wait_ge(dsts_out, 16)
            for j in range(PRE):
                stage(j, j, None)
            with pool.Fori(1, WINDOWS - 1) as i:
                for j in range(PRE):
                    stage(i * PRE + j, j, i * PRE + j + 1 - PRE)
            for j in range(PRE - 1):
                s = (WINDOWS - 1) * PRE + j
                stage(s, j, s + 1 - PRE)

            pool.wait_ge(rec_in, 32 * Q)
            for b, n in ((0, SWEEPS + 2), (1, SWEEPS)):
                pool.wait_ge(h_st[b], 16 * n)
            pool.wait_ge(sd_done, STEPS)

            def gather(q, z, cond):
                if cond is not None:
                    pool.wait_ge(idx_made, q + 1)
                pool.nop(nofuse=True)
                for g in range(Q):
                    if cond is not None:
                        pool.wait_ge(p_mm, cond + g)
                        pool.nop(nofuse=True)
                    for t in range(T):
                        nc.gpsimd.indirect_dma_start(G[:, z, g * T + t, 0:ROW], None, table,
                                                     bass.IndirectOffsetOnAxis(ap=idx[:, z, g * T + t:g * T + t + 1], axis=0)).then_inc(gath[z][g], 16)
            for z in range(SLOTS):
                nc.gpsimd.tensor_copy(idx[:, z, :].rearrange("p (g t) -> p g t", g=Q), rec[:, z * Q:(z + 1) * Q, :, 0]).then_inc(idx_made, 1)
            pool.wait_ge(idx_made, SLOTS)
            for z in range(SLOTS):
                gather(z, z, None)
            with pool.Fori(1, QUADS // SLOTS) as i:
                for z in range(SLOTS):
                    gather(i * SLOTS + z, z, (i * SLOTS + z - SLOTS) * Q + 1)
            gather(QUADS - 1, 0, (QUADS - 1 - SLOTS) * Q + 1)

            pool.wait_ge(xres_in, 32)
            for c in range(EARLY):
                w0, n = PARTS[c]
                cs = slice(w0, w0 + n)
                pool.wait_ge(rd_made, 2 * c + 2)
                a = accW[:, cs, :, 0:D].rearrange("p w h d -> p (w h) d")
                nc.gpsimd.tensor_tensor(a, a, rden[:, cs, :].rearrange("p w h -> p (w h)").unsqueeze(2).to_broadcast([P, n * H, D]),
                                        ALU.mult).then_inc(y_made, 1)
                pool.wait_ge(y_made, c + 1)
                x_ = xres[:, cs, :].rearrange("p w (h d) -> p (w h) d", h=H)
                nc.gpsimd.tensor_tensor(x_, a, x_, ALU.add).then_inc(ysum_made, 1)
            pool.wait_ge(shift_made, 1)
            for w in range(PARTS[2][0], PARTS[EARLY][0]):
                nc.gpsimd.tensor_scalar(xres[:, w, :], xres[:, w, :], rstd[:, w:w + 1], shift[:, w:w + 1], ALU.mult, ALU.add).then_inc(o_pool, 1)

        @block.tensor
        def _(pe):
            HI_LO = ((0, 0), (0, 1), (1, 0))

            pe.wait_ge(consts, 5)
            pe.wait_ge(flag_steps, 4)
            nc.tensor.matmul(psE[0][0:1, 2 * P:2 * P + 2], ones[0:GROUPS, 0:1], bad[:, :], start=True, stop=True).then_inc(bad_mm, 1)
            pe.wait_ge(w_in, 16 * R)
            pe.wait_ge(bd_made, 2)
            for r in range(R):
                if r == R // 2:
                    pe.wait_ge(cmp_made, 1)
                    nc.tensor.matmul(psE[0][:, 0:STEPS], ones[0:GROUPS, :], cmp[:, :], start=True, stop=True).then_inc(cnt_mm, 1)
                    nc.tensor.matmul(psE[0][0:STEPS, P:P + 1], cmp[:, :], ones[0:GROUPS, 0:1], start=True, stop=True).then_inc(cnt_mm, 1)
                for k in range(KT):
                    for a in range(2):
                        mm = nc.tensor.matmul(psE[1][:, (k * R + r) * 16:(k * R + r) * 16 + 16],
                                              Wnat[:, 2 * r + a, k * P:(k + 1) * P], Bd[:, a, :], start=a == 0, stop=a == 1)
            mm.then_inc(a_mm, 1)
            pe.wait_ge(a_lo, 4)
            pe.wait_ge(tabs, 1)
            pe.wait_ge(gcol_made, 1)

            def turn_W(c):
                if c >= 4:
                    pe.wait_ge(wt_lo, c - 3)
                for k in range(KT):
                    mm = nc.tensor.transpose(psH[c % 4][:, k * P:(k + 1) * P], Wnat[:, c, k * P:(k + 1) * P], ident[:, :])
                mm.then_inc(wt_mm, 1)

            def turn_x(n, b, cb, j):
                if not (isinstance(n, int) and n < 2):
                    pe.wait_ge(xt_lo, n - 1)
                for k in range(KT):
                    mm = nc.tensor.transpose(psX[b][:, k * P:(k + 1) * P], xin[:, cb, j, k * P:(k + 1) * P], ident[:, :])
                mm.then_inc(xt_mm, 1)

            def score(n, b, cb, j):
                pe.wait_ge(xt_lo, n + 1)
                if not (isinstance(n, int) and n < 2):
                    pe.wait_ge(sd_lo, n - 1)
                    pe.wait_ge(ssrc_out, n - 1)
                for k in range(KT):
                    for m, (xp, ap) in enumerate(HI_LO):
                        mm = nc.tensor.matmul(psE[b][:, 256:384], xTs[:, cb, j, xp, k * P:(k + 1) * P], A[ap][:, k, :],
                                              start=k + m == 0, stop=k == KT - 1 and m == 2)
                mm.then_inc(sc_mm, 1)

            def chunk(c, cb, landed, tiles=C):
                pe.wait_ge(x_in[cb], landed)
                for j in range(tiles):
                    turn_x(c * C + j, j % 2, cb, j)
                    if isinstance(c, int) and c < 2:
                        turn_W((c * C + j) * 2)
                        turn_W((c * C + j) * 2 + 1)
                    if j:
                        score(c * C + j - 1, (j - 1) % 2, cb, j - 1)
                score(c * C + tiles - 1, (tiles - 1) % 2, cb, tiles - 1)

            chunk(0, 0, 16)
            chunk(1, 1, 16)
            with pe.Fori(1, CHUNKS // 2) as i:
                for cb in range(2):
                    chunk(i * 2 + cb, cb, i * 16 + 16)
            chunk(CHUNKS, 0, 16 * (CHUNKS // 2 + 1), 1)

            def sd_step(s, j, b, c, n):
                pe.wait_ge(sdw_in[j], n)
                pe.wait_ge(oht, s + 1)
                if c is not None:
                    pe.wait_ge(sdm_made, c)
                for t in range(T):
                    for m in range(3):
                        mm = nc.tensor.matmul(psE[b][0:EP, t * 64:t * 64 + 64],
                                              ohT[:, b, :].rearrange("p (e t) -> p t e", t=T)[:, t, :],
                                              sdw[:, j, m, :], start=m == 0, stop=m == 2)
                mm.then_inc(sd_mm, 1)

            def table_tile(i, b, landed, steps, hcond, first):
                pe.wait_ge(xT_in[b], landed)
                done = 0
                for c in range(4):
                    if hcond is not None:
                        pe.wait_ge(h_out, hcond + c)
                    for k in range(KT):
                        for m, (xp, wp) in enumerate(HI_LO):
                            mm = nc.tensor.matmul(psH[c][:, :], xT[:, b, xp, k, :], WT[wp][:, k, c * 512:c * 512 + 512],
                                                  start=k + m == 0, stop=k == KT - 1 and m == 2)
                    mm.then_inc(h_mm, 1)
                    for j in range(c, c + 1 + c // 3) if steps == PRE else range(steps if c == 3 else 0):
                        if j < steps:
                            sd_step(i * PRE + j, j, (b + j) % 2, None if first and j < 2 else i * PRE + j - 1, i * 16 + 16)

            pe.wait_ge(wt_lo, 2 * R)
            pe.wait_ge(ssrc_out, WINDOWS)
            pe.wait_ge(sd_lo, WINDOWS)
            table_tile(0, 0, 16, PRE, None, True)
            table_tile(1, 1, 16, PRE, 1, False)
            with pe.Fori(1, SWEEPS) as i:
                for b in range(2):
                    table_tile(i * 2 + b, b, i * 16 + 16, PRE, (i * 2 + b - 1) * 4 + 1, False)
            n = WINDOWS - 1
            table_tile(n, 0, 16 * (SWEEPS + 1), PRE - 1, (n - 1) * 4 + 1, False)

            def sums(q, g, z):
                s = q * Q + g
                pe.wait_ge(oh_made, s + 1)
                pe.wait_ge(msg_made, s + 1)
                pe.wait_ge(first_made, q + 1)
                if not (isinstance(q, int) and q == 0):
                    pe.wait_ge(scaled, s - 3)
                for t in range(T):
                    mm = nc.tensor.matmul(psP[g][:, 0:GROW], onehot[:, g % 2, t, :], G[:, z, g * T + t, :],
                                          start=t == 0, stop=t == T - 1)
                mm.then_inc(p_mm, 1)

            def turn_scores(q):
                pe.wait_ge(s4_made, q + 1)
                if not (isinstance(q, int) and q == 0):
                    pe.wait_ge(sT_out, q)
                for t in range(T):
                    mm = nc.tensor.transpose(psT[:, t * P:t * P + EP], s4[:, t, :, :].rearrange("p g h -> p (g h)"), ident[0:EP, 0:EP])
                mm.then_inc(sT_mm, 1)

            def turn_max(q):
                pe.wait_ge(mT_made, q + 1)
                if not (isinstance(q, int) and q == 0):
                    pe.wait_ge(first_made, q)
                for t in range(T):
                    mm = nc.tensor.transpose(psM[0:EP, t * P:(t + 1) * P], mT[:, :].rearrange("p (e t) -> p t e", t=T)[:, t, :], ident[:, :])
                mm.then_inc(m_mm, 1)

            def quad(q, z):
                sums(q - 1, 0, z)
                turn_scores(q)
                sums(q - 1, 1, z)
                turn_max(q)
                sums(q - 1, 2, z)
                sums(q - 1, 3, z)

            pe.wait_ge(h_out, 4 * WINDOWS)
            turn_scores(0)
            turn_max(0)
            for q in range(1, SLOTS + 1):
                quad(q, q - 1)
            with pe.Fori(1, (QUADS - 1) // SLOTS) as i:
                for z in range(SLOTS):
                    quad(i * SLOTS + z + 1, z)
            for g in range(Q):
                sums(QUADS - 1, g, (QUADS - 1) % SLOTS)

        @block.scalar
        def _(act):
            def load_chunk(c, cb):
                act.dma_start(xin[:, cb, :, :], x[ds(c * C * P, C * P), :].rearrange("(j p) f -> p j f", p=P)).then_inc(x_in[cb], 16)

            for a, v in enumerate((attn_src, attn_dst)):
                act.dma_start(attn_col[:, a, :], v.rearrange("h d -> (h d)").rearrange("(a o) -> o a", a=2), allow_slow_non_contiguous=True).then_inc(attn_in, 16)
            load_chunk(0, 0)
            load_chunk(1, 1)
            def keep_W(c):
                act.wait_ge(wt_mm, c + 1)
                nc.scalar.copy(WT[0][:, :, c * P:(c + 1) * P], psH[c % 4][:, 0:256].rearrange("p (k n) -> p k n", k=KT)).then_inc(wt_hi, 1)

            act.wait_ge(a_mm, 1)
            pa = psE[1][:, 0:256].rearrange("p (k r c) -> p k r c", k=KT, r=R)
            for k in range(KT):
                nc.scalar.copy(A[0][:, k, 0:64].rearrange("p (r h) -> p r h", r=R), pa[:, k, :, 0:H]).then_inc(a_hi, 1)
                nc.scalar.copy(A[0][:, k, 64:128].rearrange("p (h r) -> p r h", r=R), pa[:, k, :, H:2 * H]).then_inc(a_hi, 1)

            def keep_xT(n, b, cb, j):
                act.wait_ge(xt_mm, n + 1)
                nc.scalar.copy(xTs[:, cb, j, 0, :], psX[b][:, 0:256]).then_inc(xt_hi, 1)

            def keep_scores(n, b, cb, j):
                act.wait_ge(sc_mm, n + 1)
                nc.scalar.copy(sdo[:, cb, j, 0, :], psE[b][:, 320:384]).then_inc(sd_hi, 1)
                nc.scalar.copy(ssrc[:, ds(n, 1), :].rearrange("p a c -> p (a c)"), psE[b][:, 256:320]).then_inc(ssrc_out, 1)

            def store_chunk(c, cb, tiles=C):
                if tiles == C:
                    act.wait_ge(xt_lo, c * C + C)
                    act.dma_start(xT_d[ds(c * C, C), :, :].rearrange("j p c -> p j c"),
                                  xTs[:, cb, :, :, :].rearrange("p j a c -> p j (a c)").bitcast(F32)).then_inc(chunk_st[cb], 16)
                    act.wait_ge(sd_parts, (c * C + C) * 2)
                    act.dma_start(sdst_d[ds(c * C, C), :, :].rearrange("j p c -> p j c"),
                                  sdo[:, cb, :, :, :].rearrange("p j a c -> p j (a c)")).then_inc(chunk_st[cb], 16)
                else:
                    act.wait_ge(xt_lo, WINDOWS)
                    act.dma_start(xT_d[WINDOWS - 1], xTs[:, cb, 0, :, :].rearrange("p a c -> p (a c)").bitcast(F32)).then_inc(chunk_st[cb], 16)
                    act.wait_ge(sd_parts, 2 * WINDOWS)
                    act.dma_start(sdst_d[WINDOWS - 1], sdo[:, cb, 0, :, :].rearrange("p a c -> p (a c)")).then_inc(chunk_st[cb], 16)

            def keep_chunk(c, cb, stored, load, tiles=C):
                if stored is not None:
                    act.wait_ge(chunk_st[cb], stored)
                for j in range(tiles):
                    keep_xT(c * C + j, j % 2, cb, j)
                    if isinstance(c, int) and c < 2:
                        keep_W((c * C + j) * 2)
                        keep_W((c * C + j) * 2 + 1)
                    if j == 0 and not (isinstance(c, int) and c == 0):
                        store_chunk(c - 1, 1 - cb)
                    if j:
                        keep_scores(c * C + j - 1, (j - 1) % 2, cb, j - 1)
                if load is not None:
                    load()
                keep_scores(c * C + tiles - 1, (tiles - 1) % 2, cb, tiles - 1)

            keep_chunk(0, 0, None, lambda: load_chunk(2, 0))
            keep_chunk(1, 1, None, lambda: load_chunk(3, 1))
            with act.Fori(1, CHUNKS // 2 - 1) as i:
                for cb in range(2):
                    keep_chunk(i * 2 + cb, cb, i * 32, lambda: load_chunk(i * 2 + cb + 2, cb))
            keep_chunk(CHUNKS - 2, 0, 32 * (CHUNKS // 2 - 1),
                       lambda: act.dma_start(xin[0:TAIL, 0, 0, :], x[(WINDOWS - 1) * P:N, :]).then_inc(x_in[0], 16))
            keep_chunk(CHUNKS - 1, 1, 32 * (CHUNKS // 2 - 1), None)
            def load_xT(n, b):
                act.dma_start(xT[:, b, :, :, :].rearrange("p a k n -> p (a k n)").bitcast(F32), xT_d[ds(n, 1), :, :].rearrange("a p c -> p (a c)")).then_inc(xT_in[b], 16)

            act.wait_ge(chunk_st[0], 32)
            load_xT(0, 0)
            load_xT(1, 1)
            keep_chunk(CHUNKS, 0, 32 * (CHUNKS // 2), None, 1)
            store_chunk(CHUNKS, 0, 1)

            def keep_tile(i, b, stored, load, rows=P):
                if stored is not None:
                    act.wait_ge(h_st[b], stored)
                nc.scalar.copy(hbuf[:, b, :, :, D], ssrc[:, ds(i, 1), :].rearrange("p a (r h) -> p (a r) h", r=R)).then_inc(hs_out, 1)
                for c in range(4):
                    act.wait_ge(h_mm, i * 4 + c + 1)
                    nc.scalar.copy(hbuf[:, b, 2 * c:2 * c + 2, :, 0:D].rearrange("p r h d -> p (r h) d"),
                                   psH[c][:, :].rearrange("p (r d) -> p r d", d=D)).then_inc(h_out, 1)
                if load is not None:
                    load_xT(i + 2, b)
                act.wait_ge(h_out, i * 4 + 4)
                act.wait_ge(hs_out, i + 1)
                for lo, hi in ((0, rows),) if rows == P else ((0, TAIL_SPRAY), (TAIL_SPRAY, TAIL)):
                    act.dma_start(table[ds(i * P * R + lo * R, (hi - lo) * R), :].rearrange("(p r) c -> p (r c)", r=R),
                                  hbuf[lo:hi, b, :, :, :].rearrange("p r h d -> p (r h d)")).then_inc(h_st[b], 16)

            act.wait_ge(ssrc_out, WINDOWS)
            for b in range(2):
                keep_tile(b, b, None, True)
            for b, n in ((0, CHUNKS // 2 + 1), (1, CHUNKS // 2)):
                act.wait_ge(chunk_st[b], 32 * n)
            with act.Fori(1, SWEEPS - 1) as i:
                for b in range(2):
                    keep_tile(i * 2 + b, b, i * 16, True)
            n = WINDOWS - 3
            keep_tile(n, 0, 16 * (SWEEPS - 1), True)
            keep_tile(n + 1, 1, 16 * (SWEEPS - 1), None)
            keep_tile(n + 2, 0, 16 * SWEEPS, None, TAIL)

            for b, n in ((0, SWEEPS + 2), (1, SWEEPS)):
                act.wait_ge(h_st[b], 16 * n)
            act.wait_ge(sd_done, STEPS)

            def keep_sT(q):
                act.wait_ge(sT_mm, q + 1)
                if not (isinstance(q, int) and q == 0):
                    act.wait_ge(fwd_made, q)
                nc.scalar.activation(sT[:, :].rearrange("p (e t) -> p e t", t=T),
                                     psT[:, :].rearrange("p (t e) -> p e t", t=T)[:, 0:EP, :], ACT.Relu).then_inc(sT_out, 1)

            def weights(q, z):
                act.wait_ge(dif_made, q + 1)
                gw = G[:, z, :, 0:ROW].rearrange("p (g t) (h d) -> p g t h d", g=Q, h=H)
                for g in range(Q):
                    i_ = nc.scalar.activation(gw[:, g, :, :, D],
                                              dif[:, :, :].rearrange("p (t g) h -> p g t h", g=Q)[:, g, :, :], ACT.Exp)
                i_.then_inc(w_made, 1)

            def shifts(q, g):
                s = q * Q + g
                b = g % 2
                act.wait_ge(dab_made, s * 2 + 4)
                act.wait_ge(acc_made, s + 1)
                nc.scalar.activation(eab[:, b, :], dab[:, b, :], ACT.Exp).then_inc(eab_made, 1)
                act.wait_ge(eab_made, s + 1)
                for h in range(H):
                    i_ = nc.scalar.activation(tsum[:, b, h * HD:(h + 1) * HD], psP[g][:, h * HD:(h + 1) * HD], ACT.Copy, scale=eab[:, b, H + h:H + h + 1])
                i_.then_inc(scaled, 1)

            def quad(q, z, before=True):
                if before:
                    shifts(q - 2, 3)
                keep_sT(q)
                shifts(q - 1, 0)
                shifts(q - 1, 1)
                weights(q, (z + 1) % SLOTS)
                shifts(q - 1, 2)

            keep_sT(0)
            weights(0, 0)
            for q in range(1, SLOTS + 1):
                quad(q, q - 1, q > 1)
            with act.Fori(1, (QUADS - 1) // SLOTS) as i:
                for z in range(SLOTS):
                    quad(i * SLOTS + z + 1, z)
            shifts(QUADS - 2, 3)
            for g in range(Q):
                shifts(QUADS - 1, g)

            act.wait_ge(shift_made, 1)
            for w in range(PARTS[2][0]):
                nc.scalar.activation(xres[:, w, :], xres[:, w, :], ACT.Identity, bias=shift[:, w:w + 1], scale=rstd[:, w:w + 1]).then_inc(o_act, 1)

        @block.vector
        def _(dve):
            v = nc.vector
            v.memset(nxt[:, :], 1 << 24).then_inc(flag_steps, 1)
            v.memset(keep[:, 0:1], 0.0).then_inc(keep_made, 1)
            dve.wait_ge(consts, 5)
            v.tensor_copy(pcol[:, :], iota_col[:, :]).then_inc(win_made, 1)
            dve.wait_ge(attn_in, 32)
            for a in range(2):
                v.tensor_tensor(Bd[:, :, a * H:(a + 1) * H], headsel[:, :, :],
                                attn_col[:, a, :].unsqueeze(2).to_broadcast([P, 2, H]), ALU.mult).then_inc(bd_made, 1)
            dve.wait_ge(edges_in, 64)
            v.tensor_tensor(neE[:, 1:GE], dstE[:, 1:GE], dstE[:, 0:GE - 1], ALU.is_lt).then_inc(flag_steps, 1)
            v.tensor_tensor(bad[:, 0:1], nxt[:, 0:1], dstE[:, GE - 1:GE], ALU.is_lt).then_inc(flag_steps, 1)
            dve.wait_ge(flag_steps, 2)
            v.tensor_reduce(bad[:, 1:2], neE[:, 1:GE], axis=AXX, op=ALU.max).then_inc(flag_steps, 1)
            dve.wait_ge(bad_mm, 1)
            v.tensor_reduce(unsorted[:, :], psE[0][0:1, 2 * P:2 * P + 2], axis=AXX, op=ALU.max).then_inc(flag_steps, 1)
            dve.wait_ge(flag_steps, 5)
            flag = dve.value_load(unsorted[0:1, 0:1], min_val=0, max_val=GROUPS)
            with dve.If(flag):
                dve.wait_ge(sort_in, 64)
                v.tensor_copy(srt[:, :, 1], own[:, :]).then_inc(srt_made, 1)
                v.tensor_scalar(thr[:, :], own[:, :], 0.5, None, ALU.add).then_inc(srt_made, 1)
                v.memset(places[:, :], 0).then_inc(srt_made, 1)
                dve.wait_ge(srt_made, 3)
                dve.wait_ge(before_made, 2)
                dve.nop(nofuse=True).then_inc(row_used, 1)

                def count(c, n):
                    dve.wait_ge(less_made, n)
                    v.tensor_reduce(less_n[:, :], less[:, :, :], axis=AXX, op=ALU.add).then_inc(less_sum, 1)
                    dve.wait_ge(less_sum, n)
                    v.tensor_tensor(places[:, c], places[:, c], less_n[:, :], ALU.add).then_inc(place_made, 1)
                    dve.wait_ge(place_made, n)
                    dve.nop(nofuse=True)

                with dve.Fori(0, GROUPS) as i:
                    dve.wait_ge(row_in, i * 16 + 16)
                    row = rowb[:, :].unsqueeze(1).to_broadcast([EP, T, GE])
                    c = ds(i * T, T)
                    v.tensor_copy(thr[:, c], own[:, c]).then_inc(thr_made, 1)
                    v.tensor_tensor(less[:, :, :], row, own[:, c].unsqueeze(2).to_broadcast([EP, T, GE]), ALU.is_equal).then_inc(thr_made, 1)
                    dve.wait_ge(thr_made, i * 2 + 2)
                    v.tensor_tensor(less[:, :, :], less[:, :, :], before[:, :, :], ALU.mult).then_inc(less_made, 1)
                    count(c, i * (GROUPS + 1) + 1)
                    with dve.Fori(0, GROUPS) as j:
                        k = ds(j * T, T)
                        v.tensor_tensor(less[:, :, :], row, thr[:, k].unsqueeze(2).to_broadcast([EP, T, GE]), ALU.is_lt).then_inc(less_made, 1)
                        count(k, i * (GROUPS + 1) + j + 2)
                    dve.nop(nofuse=True).then_inc(row_used, 1)
                dve.nop(nofuse=True).then_inc(column_used, 1)
                for n, column in ((2, 0), (3, 2)):
                    dve.wait_ge(sort_in, 64 * n)
                    v.tensor_copy(srt[:, :, column], own[:, :]).then_inc(column_used, 1)
                    dve.wait_ge(column_used, n)
                dve.nop(nofuse=True).then_inc(column_used, 1)
            dve.wait_ge(edges_ok, 1)
            v.tensor_scalar(wlast[:, :], dstE[:, GE - 1:GE], 7, None, ALU.arith_shift_right).then_inc(last_made, 1)
            v.tensor_tensor(neE[:, 1:GE], dstE[:, 1:GE], dstE[:, 0:GE - 1], ALU.not_equal).then_inc(ne_made, 1)
            dve.wait_ge(last_made, 1)
            v.tensor_tensor(glast[:, :], wlast[:, :], iota_col[0:GROUPS, :], ALU.add).then_inc(last_made, 1)
            v.memset(recE[:, 0:1, 3:4], 1).then_inc(prep, 1)
            v.memset(brkE[:, 0, 0:1], -BIG).then_inc(prep, 1)
            v.memset(brkE[:, 1, GE - 1:GE], -BIG).then_inc(prep, 1)
            dve.wait_ge(last_made, 2)
            v.tensor_scalar(cmp[:, :], iota_row[0:GROUPS, 0:STEPS], glast[:, 0:1], None, ALU.is_gt).then_inc(cmp_made, 1)
            v.scalar_tensor_tensor(out=recE[:, :, 0], in0=srcE[:, :], scalar=float(R), in1=typE[:, :], op0=ALU.mult, op1=ALU.add).then_inc(cols_made, 1)
            v.tensor_copy(recE[:, :, 1], dstE[:, :]).then_inc(cols_made, 1)
            v.tensor_copy(recE[:, :, 2], typE[:, :]).then_inc(cols_made, 1)
            dve.wait_ge(cols_made, 3)
            v.tensor_copy(dst16[:, :], dstE[:, :]).then_inc(prep, 1)
            dve.wait_ge(ne_made, 1)
            v.tensor_copy(recE[:, 1:GE, 3], neE[:, 1:GE]).then_inc(prep, 1)
            v.tensor_scalar(brkE[:, 0, 1:GE], neE[:, 1:GE], -BIG, None, ALU.mult).then_inc(prep, 1)
            v.tensor_scalar(brkE[:, 1, 0:GE - 1], neE[:, 1:GE], -BIG, None, ALU.mult).then_inc(prep, 1)
            dve.wait_ge(cnt_mm, 2)
            v.tensor_scalar(gcol[:, :], psE[0][0:STEPS, P:P + 1], float(GROUPS - 1), None, ALU.min).then_inc(gcol_made, 1)
            v.tensor_scalar(cnt[:, :], psE[0][:, 0:STEPS], float(GROUPS - 1), None, ALU.min).then_inc(tabs, 1)
            dve.wait_ge(tabs, 1)
            v.tensor_tensor(win[:, :], iota_row[:, 0:STEPS], cnt[:, :], ALU.subtract).then_inc(win_made, 1)
            dve.wait_ge(win_made, 2)
            v.tensor_copy(wtab[:, :], win[0:1, :]).then_inc(tabs, 1)
            v.tensor_scalar(node[:, :], win[:, :], float(P), pcol[:, 0:1], ALU.mult, ALU.add).then_inc(tabs, 1)
            v.tensor_scalar(win128[:, :], win[:, :], float(P), None, ALU.mult).then_inc(tabs, 1)
            v.tensor_tensor(keep[:, 1:STEPS], win[:, 1:STEPS], win[:, 0:STEPS - 1], ALU.is_equal).then_inc(keep_made, 1)

            def low_W(c):
                dve.wait_ge(wt_hi, c + 1)
                v.tensor_tensor(WT[1][:, :, c * P:(c + 1) * P], psH[c % 4][:, 0:256].rearrange("p (k n) -> p k n", k=KT),
                                WT[0][:, :, c * P:(c + 1) * P].bitcast(F32), ALU.subtract).then_inc(wt_lo, 1)

            dve.wait_ge(a_hi, 4)
            pa = psE[1][:, 0:256].rearrange("p (k r c) -> p k r c", k=KT, r=R)
            for k in range(KT):
                for lo, form, a in ((0, "p (r h) -> p r h", 0), (64, "p (h r) -> p r h", 1)):
                    v.tensor_tensor(A[1][:, k, lo:lo + 64].rearrange(form, r=R), pa[:, k, :, a * H:(a + 1) * H],
                                    A[0][:, k, lo:lo + 64].bitcast(F32).rearrange(form, r=R), ALU.subtract).then_inc(a_lo, 1)

            def low_xT(n, b, cb, j):
                dve.wait_ge(xt_hi, n + 1)
                v.tensor_tensor(xTs[:, cb, j, 1, :], psX[b][:, 0:256], xTs[:, cb, j, 0, :].bitcast(F32), ALU.subtract).then_inc(xt_lo, 1)

            def low_scores(n, b, cb, j):
                dve.wait_ge(ssrc_out, n + 1)
                if not (isinstance(n, int) and n < 2):
                    dve.wait_ge(sd_parts, (n - 1) * 2)
                v.tensor_tensor(sdr[:, b, :], psE[b][:, 320:384], sdo[:, cb, j, 0, :], ALU.subtract).then_inc(sd_lo, 1)
                dve.wait_ge(sd_lo, n + 1)
                v.tensor_copy(sdo[:, cb, j, 1, :], sdr[:, b, :]).then_inc(sd_parts, 1)
                dve.wait_ge(sd_parts, n * 2 + 1)
                v.tensor_tensor(sdo[:, cb, j, 2, :], sdr[:, b, :], sdo[:, cb, j, 1, :], ALU.subtract).then_inc(sd_parts, 1)

            def low_chunk(c, cb, stored, tiles=C):
                if stored is not None:
                    dve.wait_ge(chunk_st[cb], stored)
                for j in range(tiles):
                    low_xT(c * C + j, j % 2, cb, j)
                    if isinstance(c, int) and c < 2:
                        low_W((c * C + j) * 2)
                        low_W((c * C + j) * 2 + 1)
                    if j:
                        low_scores(c * C + j - 1, (j - 1) % 2, cb, j - 1)
                low_scores(c * C + tiles - 1, (tiles - 1) % 2, cb, tiles - 1)

            low_chunk(0, 0, None)
            low_chunk(1, 1, None)
            with dve.Fori(1, CHUNKS // 2) as i:
                for cb in range(2):
                    low_chunk(i * 2 + cb, cb, i * 32)
            low_chunk(CHUNKS, 0, 32 * (CHUNKS // 2), 1)

            def oht_step(s, j, b, n, cond):
                dve.wait_ge(drow_in[j], n)
                if cond is not None:
                    dve.wait_ge(sd_mm, cond)
                v.tensor_scalar(ohT[:, b, :], drow[:, j, :], node[:, ds(s, 1)], None, ALU.is_equal).then_inc(oht, 1)
                v.tensor_tensor(rmask[:, b, :, :], rec[:, ds(s, 1), :, 2:3].rearrange("p a t c -> p (a t) c").to_broadcast([EP, T, R]),
                                iota_row[0:EP, 0:R].unsqueeze(1).to_broadcast([EP, T, R]), ALU.is_equal).then_inc(rm_made, 1)

            def pick_step(s, b):
                dve.wait_ge(sd_mm, s + 1)
                dve.wait_ge(rm_made, s + 1)
                v.tensor_tensor(sdm[:, b, :, :].rearrange("p (t h) r -> p t h r", t=T),
                                psE[b][0:EP, 0:256].rearrange("p (t h r) -> p t h r", t=T, h=H),
                                rmask[:, b, :, :].unsqueeze(2).to_broadcast([EP, T, H, R]), ALU.mult).then_inc(sdm_made, 1)
                dve.wait_ge(sdm_made, s + 1)
                v.tensor_reduce(sdS[:, ds(s, 1), :, :].rearrange("p a t h -> p (a t h)"), sdm[:, b, :, :],
                                axis=AXX, op=ALU.add).then_inc(sd_done, 1)

            dve.wait_ge(rec_in, 32 * Q)
            oht_step(0, 0, 0, 16, None)
            oht_step(1, 1, 1, 16, None)
            pick_step(0, 0)
            with dve.Fori(0, SWEEPS) as i:
                for j in range(2 * PRE):
                    s = i * (2 * PRE) + j + 2
                    oht_step(s, (j + 2) % PRE, j % 2, (i * 2 + (j + 2) // PRE + 1) * 16, s - 1)
                    pick_step(s - 1, (j + 1) % 2)
            for s in (STEPS - 2, STEPS - 1):
                oht_step(s, s % PRE, s % 2, (s // PRE + 1) * 16, s - 1)
                pick_step(s - 1, (s - 1) % 2)
            pick_step(STEPS - 1, 1)
            dve.wait_ge(sd_done, STEPS)
            dve.wait_ge(keep_made, 2)

            for b, n in ((0, SWEEPS + 2), (1, SWEEPS)):
                dve.wait_ge(h_st[b], 16 * n)
            v.memset(brk[:, :, :, :], 0.0).then_inc(zeroed, 1)
            v.memset(accS[:, :, :], 0.0).then_inc(acc_made, 2)
            v.memset(s4[:, :, :, :], 0.0).then_inc(zeroed, 1)
            v.memset(M[:, :, :], 0.0).then_inc(mnew, 1)
            v.memset(dab[:, :, :], 0.0).then_inc(dab_made, 2)
            dve.wait_ge(mnew, 1)
            dve.wait_ge(dab_made, 2)
            dve.wait_ge(acc_made, 2)
            v.memset(xres[:, WINDOWS - 1, :], 0.0).then_inc(zeroed, 1)
            dve.wait_ge(zeroed, 3)

            def scores(q, z, n):
                for g in range(Q):
                    dve.wait_ge(gath[z][g], n)
                if not isinstance(q, int) or q + SLOTS < QUADS:
                    v.tensor_copy(idx[:, z, :].rearrange("p (g t) -> p g t", g=Q), rec[:, ds((q + SLOTS) * Q, Q), :, 0]).then_inc(idx_made, 1)
                gs = G[:, z, :, 0:ROW].rearrange("p (g t) (h d) -> p g t h d", g=Q, h=H)
                for g in range(Q):
                    i_ = v.tensor_tensor(sraw[:, :, :].rearrange("p (t g) h -> p g t h", g=Q)[:, g, :, :], gs[:, g, :, :, D],
                                         sdS[:, ds(q * Q + g, 1), :, :].rearrange("p a t h -> p (a t) h"), ALU.add)
                i_.then_inc(sraw_made, 1)
                dve.wait_ge(sraw_made, q + 1)
                v.scalar_tensor_tensor(out=s4[:, :, :, 0:H].rearrange("p t g h -> p (t g) h"), in0=sraw[:, :, :],
                                       scalar=NEG_SLOPE, in1=sraw[:, :, :], op0=ALU.mult, op1=ALU.max).then_inc(s4_made, 1)

            def scans(q, b, n):
                dve.wait_ge(sT_out, q + 1)
                dve.wait_ge(brk_in[b], n)
                v.tensor_tensor_scan(fwd[:, :], brk[:, b, 0, :], sT[:, :], -BIG, ALU.add, ALU.max).then_inc(fwd_made, 1)
                dve.wait_ge(fwd_made, q + 1)
                if not (isinstance(q, int) and q == 0):
                    dve.wait_ge(m_mm, q)
                v.tensor_tensor_scan(mT[:, ::-1], brk[:, b, 1, ::-1], fwd[:, ::-1], -BIG, ALU.add, ALU.max).then_inc(mT_made, 1)

            def shifted(q, z):
                dve.wait_ge(m_mm, q + 1)
                pm = psM[0:EP, :].rearrange("p (c h) -> p c h", h=PAD)[:, :, 0:H]
                if not (isinstance(q, int) and q == 0):
                    dve.wait_ge(w_made, q)
                v.tensor_tensor(dif[:, :, :], s4[:, :, :, 0:H].rearrange("p t g h -> p (t g) h"), pm, ALU.subtract).then_inc(dif_made, 1)
                v.tensor_tensor(G[:, z, :, ROW:GROW].rearrange("p (g t) h -> p g t h", g=Q),
                                pm.rearrange("p (t g) h -> p g t h", g=Q),
                                rec[:, ds(q * Q, Q), :, 3:4].to_broadcast([EP, Q, T, H]), ALU.mult).then_inc(first_made, 1)

            def messages(q, z, g):
                s = q * Q + g
                v.scalar_tensor_tensor(out=onehot[:, g % 2, :, :],
                                       in0=rec[:, ds(s, 1), :, 1:2].rearrange("p a t c -> p (a t) c").to_broadcast([EP, T, P]),
                                       scalar=win128[0:EP, ds(s, 1)],
                                       in1=iota_row[0:EP, :].unsqueeze(1).to_broadcast([EP, T, P]),
                                       op0=ALU.subtract, op1=ALU.is_equal).then_inc(oh_made, 1)
                dve.wait_ge(w_made, q + 1)
                f = G[:, z, g * T:(g + 1) * T, 0:ROW].rearrange("p t (h d) -> p t h d", h=H)
                v.tensor_tensor(f[:, :, :, 0:D], f[:, :, :, 0:D], f[:, :, :, D:HD].to_broadcast([EP, T, H, D]), ALU.mult).then_inc(msg_made, 1)

            def maxima(q, g):
                s = q * Q + g
                b, o_ = g % 2, (g + 1) % 2
                dve.wait_ge(p_mm, s + 1)
                dve.wait_ge(mnew, s + 1)
                dve.wait_ge(dab_made, s * 2 + 2)
                k = keep[:, ds(s, 1)]
                ms = psP[g][:, ROW:GROW]
                v.scalar_tensor_tensor(out=M[:, b, :], in0=M[:, o_, :], scalar=k, in1=ms, op0=ALU.mult, op1=ALU.max).then_inc(mnew, 1)
                dve.wait_ge(mnew, s + 2)
                v.scalar_tensor_tensor(out=dab[:, b, 0:H], in0=M[:, o_, :], scalar=k, in1=M[:, b, :], op0=ALU.mult, op1=ALU.subtract).then_inc(dab_made, 1)
                v.tensor_tensor(dab[:, b, H:2 * H], ms, M[:, b, :], ALU.subtract).then_inc(dab_made, 1)

            def merge(q, g):
                s = q * Q + g
                b = g % 2
                dve.wait_ge(scaled, s + 1)
                dve.wait_ge(acc_made, s + 2)
                dve.wait_ge(acc_st, s * 16 + 16)
                v.scalar_tensor_tensor(out=accS[:, b, :].rearrange("p (h d) -> p h d", h=H),
                                       in0=accS[:, (g + 1) % 2, :].rearrange("p (h d) -> p h d", h=H), scalar=keep[:, ds(s, 1)],
                                       in1=eab[:, b, 0:H].unsqueeze(2).to_broadcast([P, H, HD]), op0=ALU.mult, op1=ALU.mult).then_inc(acc_scaled, 1)
                dve.wait_ge(acc_scaled, s + 1)
                v.tensor_tensor(accS[:, b, :], accS[:, b, :], tsum[:, b, :], ALU.add).then_inc(acc_made, 1)

            scores(0, 0, 16 * T)
            scans(0, 0, 16 * Q)
            shifted(0, 0)
            def quad(q, c, gathered, broken, before=True):
                zq, zp = (c + 1) % SLOTS, c % SLOTS
                messages(q - 1, zp, 0)
                if before:
                    maxima(q - 2, 3)
                    merge(q - 2, 2)
                scores(q, zq, gathered)
                messages(q - 1, zp, 1)
                maxima(q - 1, 0)
                if before:
                    merge(q - 2, 3)
                scans(q, (c + 1) % 2, broken)
                messages(q - 1, zp, 2)
                maxima(q - 1, 1)
                merge(q - 1, 0)
                shifted(q, zq)
                messages(q - 1, zp, 3)
                maxima(q - 1, 2)
                merge(q - 1, 1)

            for q in range(1, 2 * SLOTS + 1):
                quad(q, q - 1, (q // SLOTS + 1) * 16 * T, (q // 2 + 1) * 16 * Q, q > 1)
            with dve.Fori(1, (QUADS - 1) // (2 * SLOTS) - 1) as i:
                for c in range(2 * SLOTS):
                    quad(i * (2 * SLOTS) + c + 1, c, (i * 2 + (c + 1) // SLOTS + 1) * 16 * T, (i * SLOTS + (c + 1) // 2 + 1) * 16 * Q)

            def inverse(c, den=None):
                w0, n = PARTS[c]
                cs = slice(w0, w0 + n)
                if den is None:
                    dve.wait_ge(acc_st, 16 * (GROUPS - 1 + w0 + n + 2))
                    den = accW[:, cs, :, D]
                v.tensor_scalar(rden[:, cs, :], den, DENOM_EPS, None, ALU.add).then_inc(rd_made, 1)
                dve.wait_ge(rd_made, 2 * c + 1)
                v.reciprocal(rden[:, cs, :], rden[:, cs, :]).then_inc(rd_made, 1)

            def divide(c, a):
                w0, n = PARTS[c]
                dve.wait_ge(rd_made, 2 * c + 2)
                v.tensor_tensor(a, a, rden[:, w0:w0 + n, :].rearrange("p w h -> p (w h)").unsqueeze(2).to_broadcast([P, n * H, D]),
                                ALU.mult).then_inc(y_made, 1)
                dve.wait_ge(y_made, c + 1)
                dve.wait_ge(xres_in, 32)
                x_ = xres[:, w0:w0 + n, :].rearrange("p w (h d) -> p (w h) d", h=H)
                v.tensor_tensor(x_, a, x_, ALU.add).then_inc(ysum_made, 1)

            def statistics(c):
                w0, n = PARTS[c]
                dve.wait_ge(ysum_made, c + 1)
                for w in range(w0, w0 + n):
                    v.bn_stats(st[:, w, :], xres[:, w, :]).then_inc(stats_made, 1)
                dve.wait_ge(stats_made, w0 + n)
                for w in range(w0, w0 + n):
                    v.bn_aggr(mv[:, w, :], st[:, w, :]).then_inc(mv_made, 1)

            def deviations(b, w0, w1):
                ve, y, t = vare[:, w0:w1], rstd[:, w0:w1], newt[:, w0:w1]
                n = b * (3 + 3 * NEWTON)
                dve.wait_ge(mv_made, w1)
                v.tensor_scalar(ve, mv[:, w0:w1, 1], LN_EPS, None, ALU.add).then_inc(root_steps, 1)
                dve.wait_ge(root_steps, n + 1)
                v.tensor_scalar(half[:, w0:w1], ve.bitcast(I32), 1, None, ALU.arith_shift_right).then_inc(root_steps, 1)
                dve.wait_ge(root_steps, n + 2)
                v.tensor_scalar(y.bitcast(I32), half[:, w0:w1], -1.0, float(MAGIC), ALU.mult, ALU.add).then_inc(root_steps, 1)
                for k in range(1, NEWTON + 1):
                    dve.wait_ge(root_steps, n + 3 * k)
                    v.scalar_tensor_tensor(out=t, in0=y, scalar=-0.5, in1=ve, op0=ALU.mult, op1=ALU.mult).then_inc(root_steps, 1)
                    dve.wait_ge(root_steps, n + 3 * k + 1)
                    v.tensor_tensor(t, t, y, ALU.mult).then_inc(root_steps, 1)
                    dve.wait_ge(root_steps, n + 3 * k + 2)
                    v.scalar_tensor_tensor(out=y, in0=t, scalar=1.5, in1=y, op0=ALU.add, op1=ALU.mult).then_inc(root_steps, 1)
                dve.wait_ge(root_steps, n + 3 * NEWTON + 3)
                v.scalar_tensor_tensor(out=shift[:, w0:w1], in0=mv[:, w0:w1, 0], scalar=-1.0, in1=y, op0=ALU.mult, op1=ALU.mult).then_inc(shift_made, 1)

            inverted = {QUADS - 4: 0, QUADS - 2: 1, QUADS - 1: 2}
            for q in range(QUADS - 2 * SLOTS, QUADS):
                quad(q, q - 1, (q // SLOTS + 1) * 16 * T, (q // 2 + 1) * 16 * Q)
                if q in inverted:
                    inverse(inverted[q])
            zl = (QUADS - 1) % SLOTS
            messages(QUADS - 1, zl, 0)
            maxima(QUADS - 2, 3)
            merge(QUADS - 2, 2)
            messages(QUADS - 1, zl, 1)
            maxima(QUADS - 1, 0)
            merge(QUADS - 2, 3)
            inverse(3)
            messages(QUADS - 1, zl, 2)
            maxima(QUADS - 1, 1)
            merge(QUADS - 1, 0)
            statistics(0)
            messages(QUADS - 1, zl, 3)
            maxima(QUADS - 1, 2)
            merge(QUADS - 1, 1)
            statistics(1)
            maxima(QUADS - 1, 3)
            merge(QUADS - 1, 2)
            statistics(2)
            merge(QUADS - 1, 3)
            statistics(3)
            deviations(0, 0, PARTS[EARLY][0])
            inverse(4)
            divide(4, accW[:, PARTS[4][0]:PARTS[5][0], :, 0:D].rearrange("p w h d -> p (w h) d"))
            sums = accS[:, (STEPS - 1) % 2, :].rearrange("p (h d) -> p h d", h=H)
            dve.wait_ge(acc_made, STEPS + 2)
            inverse(5, sums[:, :, D].unsqueeze(1))
            divide(5, sums[:, :, 0:D])
            statistics(4)
            statistics(5)
            deviations(1, PARTS[4][0], WINDOWS)
            dve.wait_ge(shift_made, 2)
            for w in range(PARTS[4][0], WINDOWS):
                v.tensor_scalar(xres[:, w, :], xres[:, w, :], rstd[:, w:w + 1], shift[:, w:w + 1], ALU.mult, ALU.add).then_inc(o_dve, 1)


def kernel(x, src, dst, edge_type_8, L0_gnn_W, L0_gnn_attn_src, L0_gnn_attn_dst):
    import concourse.bacc as bacc
    from concourse import mybir
    from concourse.bass_utils import run_bass_kernel_spmd

    nc = bacc.Bacc("TRN2", target_bir_lowering=False, num_devices=1)
    named = {"x": x, "src": src, "dst": dst, "etype": edge_type_8, "W": L0_gnn_W,
             "attn_src": L0_gnn_attn_src, "attn_dst": L0_gnn_attn_dst}
    arrays, aps = {}, {}
    for name, a in named.items():
        a = np.ascontiguousarray(a)
        arrays[f"in_{name}"] = a
        aps[name] = nc.dram_tensor(f"in_{name}", a.shape, mybir.dt.from_np(a.dtype), kind="ExternalInput").ap()
    out = nc.dram_tensor("out_0", (N, F), mybir.dt.float32, kind="ExternalOutput").ap()
    gnn_kernel(nc, out=out, **aps)
    r = run_bass_kernel_spmd(nc, [arrays], core_ids=[0])
    return r.results[0]["out_0"]
```
